# Optimizing a Trainium2 kernel written in Bass

```python
import numpy as np
import jax
import jax.numpy as jnp

def _softmax(x, axis=-1):
    return jax.nn.softmax(x, axis=axis)

def _gelu(x):
    return jax.nn.gelu(x, approximate=True)

def _silu(x):
    return jax.nn.silu(x)

def _sigmoid(x):
    return jax.nn.sigmoid(x)

def _layernorm(x, axis=-1, eps=1e-05):
    m = jnp.mean(x, axis=axis, keepdims=True)
    v = jnp.var(x, axis=axis, keepdims=True)
    return (x - m) / jnp.sqrt(v + eps)

def _scatter_add(tgt, idx, src, axis=0):
    return tgt.at[idx].add(src)

def _segment_sum(src, seg, n):
    return jax.ops.segment_sum(src, seg, n)
kernel_name = 'mk_gnn_resnorm_d2_gnn_r8_ce1a88'

def setup_inputs(seed: int=0):
    np.random.seed(seed)
    _w = jnp.asarray

    def _rec_inputs():
        import jax
        import jax.numpy as jnp
        _gk = jax.random.key(seed)
        x = -0.0003713 + 1 * jax.random.normal(jax.random.fold_in(_gk, 1), (6250, 256), jnp.float32)
        _s = jax.random.randint(jax.random.fold_in(_gk, 2), (100000,), 0, 6250, jnp.int32)
        _d = jax.random.randint(jax.random.fold_in(_gk, 3), (100000,), 0, 6250, jnp.int32)
        _loop = jnp.arange(6250, dtype=jnp.int32)
        src = jnp.concatenate([_s, _d, _loop])
        dst = jnp.concatenate([_d, _s, _loop])
        _o = jnp.argsort(dst, stable=True)
        src = src[_o]
        dst = dst[_o]
        edge_attr_128 = -0.000128692 + 0.999872 * jax.random.normal(jax.random.fold_in(_gk, 12), (206250, 128), jnp.float32)
        edge_attr_64 = -5.3897e-05 + 0.999841 * jax.random.normal(jax.random.fold_in(_gk, 13), (206250, 64), jnp.float32)
        return (x, src, dst, edge_attr_128, edge_attr_64)
    x, src, dst, edge_attr_128, edge_attr_64 = _rec_inputs()

    def _L0_gnn_setup():
        import jax, jax.numpy as jnp
        import numpy as np
        N_NODES = 6250
        N_EDGES = 50000
        D_NODE = 256
        D_EDGE = 64
        LN_EPS = 1e-06

        def _layer_norm(x, scale, bias):
            mu = jnp.mean(x, axis=-1, keepdims=True)
            var = jnp.mean(jnp.square(x - mu), axis=-1, keepdims=True)
            return (x - mu) * jax.lax.rsqrt(var + LN_EPS) * scale + bias

        def _glorot(key, shape):
            fan_in, fan_out = shape
            std = jnp.sqrt(2.0 / (fan_in + fan_out))
            return std * jax.random.normal(key, shape, dtype=jnp.float32)

        def _relu_mlp_skip(x, Ws, bs):
            n = len(Ws)
            for i, (W, b) in enumerate(zip(Ws, bs)):
                y = x @ W + b
                if i < n - 1:
                    y = jax.nn.relu(y)
                x = x + y if y.shape[-1] == x.shape[-1] else y
            return x
        key = jax.random.key(seed)
        ks = jax.random.split(key, 10)
        inp = {'nodes': jax.random.normal(ks[0], (N_NODES, D_NODE), dtype=jnp.float32), 'edges': jax.random.normal(ks[1], (N_EDGES, D_EDGE), dtype=jnp.float32), 'senders': jax.random.randint(ks[2], (N_EDGES,), 0, N_NODES, dtype=jnp.int32), 'receivers': jax.random.randint(ks[3], (N_EDGES,), 0, N_NODES, dtype=jnp.int32), 'W_message': _glorot(ks[4], (D_NODE + D_EDGE, D_NODE)), 'mlp_W0': _glorot(ks[5], (D_NODE, D_NODE)), 'mlp_b0': jnp.zeros((D_NODE,), jnp.float32), 'mlp_W1': _glorot(ks[6], (D_NODE, D_NODE)), 'mlp_b1': jnp.zeros((D_NODE,), jnp.float32), 'mlp_W2': _glorot(ks[7], (D_NODE, D_NODE)), 'mlp_b2': jnp.zeros((D_NODE,), jnp.float32), 'ln_aggr_scale': jnp.ones((D_NODE,), jnp.float32), 'ln_aggr_bias': jnp.zeros((D_NODE,), jnp.float32), 'ln_out_scale': jnp.ones((D_NODE,), jnp.float32), 'ln_out_bias': jnp.zeros((D_NODE,), jnp.float32)}
        return inp
    _L0_gnn_all = _L0_gnn_setup()
    _L0_gnn_in = {k: v for k, v in _L0_gnn_all.items() if k in ('W_message', 'mlp_W0', 'mlp_b0', 'mlp_W1', 'mlp_b1', 'mlp_W2', 'mlp_b2', 'ln_aggr_scale', 'ln_aggr_bias', 'ln_out_scale', 'ln_out_bias')}
    del _L0_gnn_all

    def _L1_gnn_setup():
        import jax, jax.numpy as jnp
        import numpy as np
        SLOPE = 0.2
        N_NODES = 1250
        N_EDGES = 40000
        D_NODE = 256
        D_EDGE = 128
        D_HID = 256
        key = jax.random.key(seed)
        ks = jax.random.split(key, 10)
        node_features = jax.random.normal(ks[0], (N_NODES, D_NODE), dtype=jnp.float32)
        edge_features = jax.random.normal(ks[1], (N_EDGES, D_EDGE), dtype=jnp.float32)
        edge_index = jax.random.randint(ks[2], (2, N_EDGES), 0, N_NODES, dtype=jnp.int64)

        def lin(k, fan_in, fan_out):
            lim = 1.0 / np.sqrt(fan_in)
            kw, kb = jax.random.split(k)
            W = jax.random.uniform(kw, (fan_in, fan_out), minval=-lim, maxval=lim, dtype=jnp.float32)
            b = jax.random.uniform(kb, (fan_out,), minval=-lim, maxval=lim, dtype=jnp.float32)
            return (W, b)
        w_W, w_b = lin(ks[3], D_NODE, D_HID)
        ew_W, ew_b = lin(ks[4], D_EDGE, D_HID)
        a_W, a_b = lin(ks[5], 3 * D_HID, 1)
        return {'node_features': node_features, 'edge_features': edge_features, 'edge_index': edge_index, 'w_W': w_W, 'w_b': w_b, 'ew_W': ew_W, 'ew_b': ew_b, 'a_W': a_W, 'a_b': a_b}
    _L1_gnn_all = _L1_gnn_setup()
    _L1_gnn_in = {k: v for k, v in _L1_gnn_all.items() if k in ('w_W', 'w_b', 'ew_W', 'ew_b', 'a_W', 'a_b')}
    del _L1_gnn_all
    return {'x': x, 'src': src, 'dst': dst, 'edge_attr_128': edge_attr_128, 'edge_attr_64': edge_attr_64, 'L0_gnn_W_message': _L0_gnn_in['W_message'], 'L0_gnn_mlp_W0': _L0_gnn_in['mlp_W0'], 'L0_gnn_mlp_b0': _L0_gnn_in['mlp_b0'], 'L0_gnn_mlp_W1': _L0_gnn_in['mlp_W1'], 'L0_gnn_mlp_b1': _L0_gnn_in['mlp_b1'], 'L0_gnn_mlp_W2': _L0_gnn_in['mlp_W2'], 'L0_gnn_mlp_b2': _L0_gnn_in['mlp_b2'], 'L0_gnn_ln_aggr_scale': _L0_gnn_in['ln_aggr_scale'], 'L0_gnn_ln_aggr_bias': _L0_gnn_in['ln_aggr_bias'], 'L0_gnn_ln_out_scale': _L0_gnn_in['ln_out_scale'], 'L0_gnn_ln_out_bias': _L0_gnn_in['ln_out_bias'], 'L1_gnn_w_W': _L1_gnn_in['w_W'], 'L1_gnn_w_b': _L1_gnn_in['w_b'], 'L1_gnn_ew_W': _L1_gnn_in['ew_W'], 'L1_gnn_ew_b': _L1_gnn_in['ew_b'], 'L1_gnn_a_W': _L1_gnn_in['a_W'], 'L1_gnn_a_b': _L1_gnn_in['a_b']}

def reference(x, src, dst, edge_attr_128, edge_attr_64, L0_gnn_W_message, L0_gnn_mlp_W0, L0_gnn_mlp_b0, L0_gnn_mlp_W1, L0_gnn_mlp_b1, L0_gnn_mlp_W2, L0_gnn_mlp_b2, L0_gnn_ln_aggr_scale, L0_gnn_ln_aggr_bias, L0_gnn_ln_out_scale, L0_gnn_ln_out_bias, L1_gnn_w_W, L1_gnn_w_b, L1_gnn_ew_W, L1_gnn_ew_b, L1_gnn_a_W, L1_gnn_a_b):
    import jax
    import jax.numpy as jnp

    def _L0_gnn_ref(nodes, edges, senders, receivers, W_message, mlp_W0, mlp_b0, mlp_W1, mlp_b1, mlp_W2, mlp_b2, ln_aggr_scale, ln_aggr_bias, ln_out_scale, ln_out_bias):
        import jax, jax.numpy as jnp
        import numpy as np
        N_NODES = 6250
        N_EDGES = 50000
        D_NODE = 256
        D_EDGE = 64
        LN_EPS = 1e-06

        def _layer_norm(x, scale, bias):
            mu = jnp.mean(x, axis=-1, keepdims=True)
            var = jnp.mean(jnp.square(x - mu), axis=-1, keepdims=True)
            return (x - mu) * jax.lax.rsqrt(var + LN_EPS) * scale + bias

        def _glorot(key, shape):
            fan_in, fan_out = shape
            std = jnp.sqrt(2.0 / (fan_in + fan_out))
            return std * jax.random.normal(key, shape, dtype=jnp.float32)

        def _relu_mlp_skip(x, Ws, bs):
            n = len(Ws)
            for i, (W, b) in enumerate(zip(Ws, bs)):
                y = x @ W + b
                if i < n - 1:
                    y = jax.nn.relu(y)
                x = x + y if y.shape[-1] == x.shape[-1] else y
            return x
        total_nodes = nodes.shape[0]
        sender_features = nodes[senders]
        msg_in = jnp.concatenate([sender_features, edges], axis=-1)
        messages = msg_in @ W_message
        agg = jax.ops.segment_sum(messages, receivers, num_segments=total_nodes)
        h = _layer_norm(jax.nn.relu(agg) + nodes, ln_aggr_scale, ln_aggr_bias)
        nodes_out = _relu_mlp_skip(h, [mlp_W0, mlp_W1, mlp_W2], [mlp_b0, mlp_b1, mlp_b2])
        nodes_new = _layer_norm(nodes + nodes_out, ln_out_scale, ln_out_bias)
        return nodes_new

    def _L1_gnn_ref(node_features, edge_features, edge_index, w_W, w_b, ew_W, ew_b, a_W, a_b):
        import jax, jax.numpy as jnp
        import numpy as np
        SLOPE = 0.2
        N_NODES = 1250
        N_EDGES = 40000
        D_NODE = 256
        D_EDGE = 128
        D_HID = 256
        N = node_features.shape[0]
        lrelu = lambda x: jax.nn.leaky_relu(x, negative_slope=SLOPE)
        h = lrelu(node_features @ w_W + w_b)
        edge_h = lrelu(edge_features @ ew_W + ew_b)
        tgt = edge_index[0]
        nbr = edge_index[1]
        h_i = h[tgt]
        h_j = h[nbr]
        e_ij = jnp.concatenate([h_i, h_j, edge_h], axis=-1) @ a_W + a_b
        seg_max = jax.ops.segment_max(e_ij, tgt, num_segments=N)
        ex = jnp.exp(e_ij - seg_max[tgt])
        seg_sum = jax.ops.segment_sum(ex, tgt, num_segments=N)
        alpha = ex / seg_sum[tgt]
        msg = alpha * h_j
        out = jax.ops.segment_sum(msg, tgt, num_segments=N)
        return lrelu(out)
    edge_index = jnp.stack([src, dst])
    x = _layernorm(x + _L0_gnn_ref(x, edge_attr_64, src, dst, L0_gnn_W_message, L0_gnn_mlp_W0, L0_gnn_mlp_b0, L0_gnn_mlp_W1, L0_gnn_mlp_b1, L0_gnn_mlp_W2, L0_gnn_mlp_b2, L0_gnn_ln_aggr_scale, L0_gnn_ln_aggr_bias, L0_gnn_ln_out_scale, L0_gnn_ln_out_bias), axis=-1)
    x = _layernorm(x + _L1_gnn_ref(x, edge_attr_128, edge_index, L1_gnn_w_W, L1_gnn_w_b, L1_gnn_ew_W, L1_gnn_ew_b, L1_gnn_a_W, L1_gnn_a_b), axis=-1)
    return x

_drawn_inputs = setup_inputs


def setup_inputs(seed=0):
    import zlib

    import numpy as np

    out = dict(_drawn_inputs(seed))
    spreads = {'L0_gnn_mlp_b0': (0.0, 0.276),
     'L0_gnn_mlp_b1': (0.0, 0.342),
     'L0_gnn_mlp_b2': (0.0, 0.336),
     'L0_gnn_ln_aggr_scale': (1.0, 0.2),
     'L0_gnn_ln_aggr_bias': (0.0, 0.1),
     'L0_gnn_ln_out_scale': (1.0, 0.2),
     'L0_gnn_ln_out_bias': (0.0, 0.1)}
    factors = {'edge_attr_128': 6.929, 'L1_gnn_ew_W': 7.481, 'L1_gnn_ew_b': 37.354, 'L1_gnn_a_W': 5.187}
    for name, (base, spread) in spreads.items():
        noise = np.random.default_rng([zlib.crc32(name.encode()), seed]).standard_normal(out[name].shape)
        drawn = base * np.exp(spread * noise) if base else spread * noise
        out[name] = jnp.asarray(drawn.astype(out[name].dtype))
    for name, factor in factors.items():
        out[name] = (out[name] * factor).astype(out[name].dtype)
    return out
```

```python
from contextlib import ExitStack

import concourse.bass as bass
from concourse import mybir

ALU = mybir.AluOpType
ACT = mybir.ActivationFunctionType
F32 = mybir.dt.float32
BF16 = mybir.dt.bfloat16
I32 = mybir.dt.int32
U32 = mybir.dt.uint32
U16 = mybir.dt.uint16
AX = mybir.AxisListType

P = 128
GA = 4
GC = 8
SLOPE = 0.2
LN_EPS = 1e-6
RES_EPS = 1e-5
MASKED = -1e38
LOWEST = -1e37
REC = 4


def sizes(n_nodes, n_edges):
    tiles = -(-n_edges // P)
    tiles = -(-tiles // GA) * GA
    blocks = -(-n_nodes // P)
    groups = tiles // GA
    buckets = blocks + 1
    bucket_groups = tiles * P // (GC * P) + 1 + buckets
    return dict(tiles=tiles, blocks=blocks, groups=groups, gp=-(-groups // P), rec_tiles=bucket_groups * GC)


def build(nc, a, n_nodes, n_edges, debug=None):
    z = sizes(n_nodes, n_edges)
    NT, NB, NG, GP, RT = z["tiles"], z["blocks"], z["groups"], z["gp"], z["rec_tiles"]
    NH = NB + 1
    D = a["x"].shape[1]
    DE0 = a["edge64"].shape[2]
    W0 = D + DE0
    KC = D // P
    HW = D + 2
    PER = NT // GA // NB
    FAR = 4096.0

    nodetab = nc.dram_tensor("nodetab", [NB * P, HW], F32, kind="Internal").ap()
    recs = nc.dram_tensor("recs", [P * RT, REC], I32, kind="Internal").ap()
    recs_pt = recs.rearrange("(p t) w -> p t w", t=RT)

    with ExitStack() as top:
        def sb(name, shape, dt=F32, ctx=top):
            return ctx.enter_context(nc.sbuf_tensor(name, shape, dt))

        def sem(name, ctx=top):
            return ctx.enter_context(nc.semaphore(name))

        banks = [top.enter_context(nc.psum_tensor(f"bank{i}", [P, 512], F32)) for i in range(8)]

        opened = sem("opened")

        def wait_alone(eng, *waits):
            waits = [(on, eng.to_reg(count)) for on, count in waits]
            eng.wait_ge(opened, 1)
            for on, count in waits:
                eng.wait_ge(on, count)

        iota = sb("iota", [P, P])
        lane = sb("lane", [P, 1])
        ident = sb("ident", [P, P])
        ones = sb("ones", [P, P])
        zeros_bf = sb("zeros_bf", [P, 512], BF16)
        a_start = sb("a_start", [P, NB], I32)
        a_end = sb("a_end", [P, NB], I32)
        a_skip = sb("a_skip", [P, NB], I32)
        c_start = sb("c_start", [P, NH], I32)
        c_end = sb("c_end", [P, NH], I32)
        p_all = sb("p_all", [P, NB])
        x1_all = sb("x1_all", [P, NB, D])

        mid = top.enter_context(ExitStack())
        dst_f = sb("dst_f", [P, NT], F32, mid)
        src_i = sb("src_i", [P, NT], I32, mid)
        place = sb("place", [P, NT, REC], I32, mid)
        s_all = sb("s_all", [P, NB, W0], F32, mid)

        with ExitStack() as ctx:
            dst_i = sb("dst_i", [P, NT], I32, ctx)
            hi_i = sb("hi_i", [P, NT], I32, ctx)
            hi_bf = sb("hi_bf", [P, NT], BF16, ctx)
            same = sb("same", [P, NT], BF16, ctx)
            rank_h = sb("rank_h", [P, NT], F32, ctx)
            rank = sb("rank", [P, NT], F32, ctx)
            low_i = sb("low_i", [P, NT], I32, ctx)
            tot = sb("tot", [P, NH], F32, ctx)
            first = sb("first", [P, NH], F32, ctx)
            dst_g = sb("dst_g", [P, GP, GA * P], I32, ctx)
            gmin = sb("gmin", [P, GP], F32, ctx)
            gmax = sb("gmax", [P, GP], F32, ctx)
            blk_i = sb("blk_i", [P, GP], I32, ctx)
            gnum = sb("gnum", [P, GP], F32, ctx)
            gnum_i = sb("gnum_i", [P, GP], I32, ctx)
            iota_h = sb("iota_h", [P, NH], F32, ctx)
            iota_i = sb("iota_i", [P, P], I32, ctx)
            lane_i = sb("lane_i", [P, 1], I32, ctx)
            below = sb("below", [P, P], F32, ctx)
            le = sb("le", [P, NB, GP], F32, ctx)
            ge = sb("ge", [P, NB, GP], F32, ctx)
            cand = sb("cand", [P, 2, NB], F32, ctx)
            best = sb("best", [P, 2, NB], F32, ctx)
            lo = sb("lo", [P, NB], F32, ctx)
            cnt = sb("cnt", [P, NH], F32, ctx)
            cnt_i = sb("cnt_i", [P, NH], I32, ctx)
            cum = sb("cum", [P, NH], F32, ctx)
            zrow = sb("zrow", [P, NH], F32, ctx)
            blank = sb("blank", [P, RT // 8, REC], I32, ctx)
            idx_in = sem("idx_in", ctx)
            iota_done = sem("iota_done", ctx)
            dve_done = sem("dve_done", ctx)
            blank_ready = sem("blank_ready", ctx)
            blanked = sem("blanked", ctx)
            cand_ready = sem("cand_ready", ctx)
            best_ready = sem("best_ready", ctx)
            tot_ready = sem("tot_ready", ctx)
            first_ready = sem("first_ready", ctx)
            block = ctx.enter_context(nc.Block())

            @block.sync
            def _(sp):
                sp.dma_start(dst_g[:], a["dst_groups"]).then_inc(idx_in, 16)
                sp.dma_start(dst_i[:], a["dst"]).then_inc(idx_in, 16)
                sp.dma_start(src_i[:], a["src"]).then_inc(idx_in, 16)
                sp.wait_ge(blank_ready, 1)
                for j in range(8):
                    sp.dma_start(recs_pt[:, j * (RT // 8):(j + 1) * (RT // 8), :], blank[:]).then_inc(blanked, 16)
                sp.wait_ge(blanked, 8 * 16)

            @block.gpsimd
            def _(pool):
                nc.gpsimd.iota(iota_i[:], pattern=[[1, P]], base=0, channel_multiplier=0).then_inc(iota_done, 1)
                nc.gpsimd.iota(lane_i[:], pattern=[[1, 1]], base=0, channel_multiplier=1).then_inc(iota_done, 1)
                nc.gpsimd.iota(gnum_i[:], pattern=[[1, GP]], base=0, channel_multiplier=GP).then_inc(iota_done, 1)
                pool.wait_ge(cand_ready, 1)
                nc.gpsimd.partition_all_reduce(best[:].rearrange("p a b -> p (a b)"), cand[:].rearrange("p a b -> p (a b)"),
                                               P, bass.bass_isa.ReduceOp.max).then_inc(best_ready, 1)

            @block.tensor
            def _(pe):
                pe.wait_ge(tot_ready, 1)
                nc.tensor.matmul(banks[0][:, 0:NH], below[:], tot[:], start=True, stop=True)
                nc.tensor.matmul(banks[1][:, 0:NH], ones[:], tot[:], start=True, stop=True).then_inc(first_ready, 1)

            @block.vector
            def _(dve):
                done = [0]

                def link(ins):
                    done[0] += 1
                    ins.then_inc(dve_done, 1)
                    dve.wait_ge(dve_done, done[0])

                v = nc.vector
                link(v.memset(blank[:], 0))
                v.memset(blank[:, :, 0:1], 2 * P).then_inc(blank_ready, 1)
                v.memset(zrow[:], 0.0).then_inc(opened, 1)
                dve.wait_ge(opened, 1)
                link(v.memset(ones[:], 1.0))
                link(v.memset(zeros_bf[:], 0.0))
                link(v.memset(zrow[:], 0.0))
                link(v.memset(place[:], 0))
                link(v.memset(rank[:], 1.0))
                dve.wait_ge(iota_done, 3)
                link(v.tensor_copy(iota[:], iota_i[:]))
                link(v.tensor_copy(lane[:], lane_i[:]))
                link(v.tensor_copy(gnum[:], gnum_i[:]))
                link(v.tensor_copy(iota_h[:], iota_i[:, 0:NH]))
                link(v.tensor_scalar(ident[:], iota[:], lane[:, 0:1], None, ALU.is_equal))
                link(v.tensor_scalar(below[:], iota[:], lane[:, 0:1], None, ALU.is_gt))

                dve.wait_ge(idx_in, 3 * 16)
                link(v.tensor_reduce(gmin[:], dst_g[:], AX.X, ALU.min))
                link(v.tensor_reduce(gmax[:], dst_g[:], AX.X, ALU.max))
                for g in (gmin, gmax):
                    link(v.tensor_copy(blk_i[:], g[:]))
                    link(v.tensor_scalar(blk_i[:], blk_i[:], 7, None, ALU.logical_shift_right))
                    link(v.tensor_copy(g[:], blk_i[:]))

                def over_blocks(t):
                    return t.unsqueeze(1).to_broadcast([P, NB, GP])

                d_all = iota_h[:, 0:NB].unsqueeze(2).to_broadcast([P, NB, GP])
                link(v.tensor_tensor(le[:], over_blocks(gmin[:]), d_all, ALU.is_le))
                link(v.tensor_tensor(ge[:], over_blocks(gmax[:]), d_all, ALU.is_ge))
                link(v.tensor_tensor(le[:], le[:], ge[:], ALU.mult))
                link(v.tensor_scalar(gmin[:], gnum[:], 1.0, None, ALU.add))
                link(v.tensor_scalar(gmax[:], gnum[:], -1.0, FAR, ALU.mult, ALU.add))
                link(v.tensor_tensor(ge[:], le[:], over_blocks(gmin[:]), ALU.mult))
                link(v.tensor_reduce(cand[:, 0, :], ge[:], AX.X, ALU.max))
                link(v.tensor_tensor(ge[:], le[:], over_blocks(gmax[:]), ALU.mult))
                link(v.tensor_reduce(cand[:, 1, :], ge[:], AX.X, ALU.max))
                v.memset(lo[:], 0.0).then_inc(cand_ready, 1)
                dve.wait_ge(best_ready, 1)
                link(v.tensor_scalar(lo[:], best[:, 1, :], -1.0, FAR, ALU.mult, ALU.add))
                link(v.tensor_scalar(lo[:], lo[:], float(NG - 1), None, ALU.min))
                link(v.tensor_tensor(cnt[:, 0:NB], best[:, 0, :], lo[:], ALU.subtract))
                link(v.tensor_scalar(cnt[:, 0:NB], cnt[:, 0:NB], 1.0, None, ALU.max))
                link(v.tensor_tensor_scan(cum[:, 0:NB], cnt[:, 0:NB], zrow[:, 0:NB], 0.0, ALU.add, ALU.add))
                link(v.tensor_copy(a_end[:], cum[:, 0:NB]))
                link(v.tensor_tensor(cum[:, 0:NB], cum[:, 0:NB], cnt[:, 0:NB], ALU.subtract))
                link(v.tensor_copy(a_start[:], cum[:, 0:NB]))
                link(v.tensor_tensor(lo[:], lo[:], cum[:, 0:NB], ALU.subtract))
                link(v.tensor_scalar(a_skip[:], lo[:], FAR, None, ALU.add))

                link(v.tensor_copy(dst_f[:], dst_i[:]))
                link(v.tensor_copy(place[:, :, 1], dst_i[:]))
                link(v.tensor_scalar(hi_i[:], src_i[:], 7, None, ALU.logical_shift_right))
                link(v.tensor_scalar(place[:, :, 0], src_i[:], P - 1, None, ALU.bitwise_and))
                link(v.tensor_copy(hi_bf[:], hi_i[:]))

                base = done[0]
                with dve.Fori(0, NH) as h:
                    v.tensor_scalar(same[:], hi_bf[:], iota_h[:, bass.ds(h, 1)], None, ALU.is_equal).then_inc(dve_done, 1)
                    dve.wait_ge(dve_done, h * 2 + (base + 1))
                    v.tensor_reduce(tot[:, bass.ds(h, 1)], same[:], AX.X, ALU.add).then_inc(dve_done, 1)
                    dve.wait_ge(dve_done, h * 2 + (base + 2))
                done[0] = base + 2 * NH
                v.memset(cnt[:], 0.0).then_inc(tot_ready, 1)
                dve.wait_ge(first_ready, 1)
                link(v.tensor_scalar(cnt[:], banks[1][:, 0:NH], float(GC * P - 1), None, ALU.add))
                link(v.tensor_copy(cnt_i[:], cnt[:]))
                shift = (GC * P).bit_length() - 1
                link(v.tensor_scalar(cnt_i[:], cnt_i[:], shift, None, ALU.logical_shift_right))
                link(v.tensor_copy(cnt[:], cnt_i[:]))
                link(v.tensor_scalar(cnt[:], cnt[:], 1.0, None, ALU.max))
                link(v.tensor_tensor_scan(cum[:], cnt[:], zrow[:], 0.0, ALU.add, ALU.add))
                link(v.tensor_copy(c_end[:], cum[:]))
                link(v.tensor_tensor(cum[:], cum[:], cnt[:], ALU.subtract))
                link(v.tensor_copy(c_start[:], cum[:]))
                link(v.scalar_tensor_tensor(first[:], cum[:], float(GC * P), banks[0][:, 0:NH], ALU.mult, ALU.add))

                base2 = done[0]
                with dve.Fori(0, NH) as h:
                    v.tensor_scalar(same[:], hi_bf[:], iota_h[:, bass.ds(h, 1)], None, ALU.is_equal).then_inc(dve_done, 1)
                    dve.wait_ge(dve_done, h * 3 + (base2 + 1))
                    v.tensor_tensor_scan(rank_h[:], same[:], same[:], first[:, bass.ds(h, 1)],
                                         ALU.add, ALU.max).then_inc(dve_done, 1)
                    wait_alone(dve, (dve_done, h * 3 + (base2 + 2)))
                    v.copy_predicated(rank[:], same[:].bitcast(U16), rank_h[:]).then_inc(dve_done, 1)
                    dve.wait_ge(dve_done, h * 3 + (base2 + 3))
                done[0] = base2 + 3 * NH
                link(v.tensor_scalar(rank[:], rank[:], -1.0, None, ALU.add))
                link(v.tensor_copy(hi_i[:], rank[:]))
                link(v.tensor_scalar(low_i[:], hi_i[:], P - 1, None, ALU.bitwise_and))
                link(v.tensor_scalar(hi_i[:], hi_i[:], 7, None, ALU.logical_shift_right))
                link(v.tensor_copy(rank[:], low_i[:]))
                link(v.tensor_copy(rank_h[:], hi_i[:]))
                link(v.scalar_tensor_tensor(place[:, :, 3], rank[:], float(RT), rank_h[:], ALU.mult, ALU.add))

        if debug == "setup":
            with nc.semaphore("dbg") as dbg, nc.Block() as block:
                @block.sync
                def _(sp):
                    sp.dma_start(a["o_place"], place[:]).then_inc(dbg, 16)
                    sp.dma_start(a["o_a"], a_start[:]).then_inc(dbg, 16)
                    sp.dma_start(a["o_b"], a_end[:]).then_inc(dbg, 16)
                    sp.dma_start(a["o_c"], a_skip[:]).then_inc(dbg, 16)
                    sp.dma_start(a["o_d"], c_start[:]).then_inc(dbg, 16)
                    sp.dma_start(a["o_e"], c_end[:]).then_inc(dbg, 16)
                    sp.wait_ge(dbg, 96)
            return

        with ExitStack() as ctx:
            rows = sb("rows", [P, GA, W0], F32, ctx)
            hot = sb("hot", [P, GA, P], F32, ctx)
            nodes_here = sb("nodes_here", [P, P], F32, ctx)
            src_slot = [sb(f"src_slot{k}", [P, 1], I32, ctx) for k in range(GA)]
            idx_ready = [sem(f"idx_ready{k}", ctx) for k in range(GA)]
            x_in = [sem(f"x_in{k}", ctx) for k in range(GA)]
            e_in = [sem(f"e_in{k}", ctx) for k in range(GA)]
            summed = [sem(f"summed{k}", ctx) for k in range(GA)]
            hot_ready = sem("hot_ready", ctx)
            nodes_ready = sem("nodes_ready", ctx)
            s_kept = sem("s_kept", ctx)
            block = ctx.enter_context(nc.Block())
            s_ps = banks[0]

            def span(eng, d):
                col = bass.ds(d, 1)
                lo = eng.value_load(a_start[0:1, col], min_val=0, max_val=NG * NB)
                hi = eng.value_load(a_end[0:1, col], min_val=1, max_val=NG * NB)
                skip = eng.value_load(a_skip[0:1, col], min_val=0, max_val=2 * int(FAR))
                return lo, hi, skip

            def tile_of(i, skip, k):
                group = (i + skip - int(FAR)).with_bounds(min_val=0, max_val=NG - 1)
                return group * GA + k

            @block.sync
            def _(sp):
                with sp.Fori(0, NB) as d:
                    lo, hi, skip = span(sp, d)
                    with sp.Fori(lo, hi) as i:
                        for k in range(GA):
                            sp.wait_ge(summed[k], i)
                            sp.dma_start(rows[:, k, D:W0],
                                         a["edge64"][:, bass.ds(tile_of(i, skip, k), 1), :]).then_inc(e_in[k], 16)

            @block.gpsimd
            def _(pool):
                with pool.Fori(0, NB) as d:
                    lo, hi, skip = span(pool, d)
                    with pool.Fori(lo, hi) as i:
                        for k in range(GA):
                            wait_alone(pool, (idx_ready[k], i + 1), (summed[k], i))
                            pool.indirect_dma_start(
                                out=rows[:, k, 0:D], out_offset=None, in_=a["x"],
                                in_offset=bass.IndirectOffsetOnAxis(ap=src_slot[k][:].bitcast(U32), axis=0),
                            ).then_inc(x_in[k], 16)

            @block.scalar
            def _(act):
                with act.Fori(0, NB) as d:
                    lo, hi, skip = span(act, d)
                    with act.Fori(lo, hi) as i:
                        for k in range(GA):
                            act.wait_ge(x_in[k], i * 16)
                            nc.scalar.copy(src_slot[k][:], src_i[:, bass.ds(tile_of(i, skip, k), 1)]).then_inc(idx_ready[k], 1)
                    act.wait_ge(summed[GA - 1], hi)
                    nc.scalar.copy(s_all[:, bass.ds(d, 1), :], s_ps[:, 0:W0].unsqueeze(1)).then_inc(s_kept, 1)

            @block.vector
            def _(dve):
                v = nc.vector
                v.tensor_scalar(nodes_here[:], iota[:], -float(P), None, ALU.add).then_inc(nodes_ready, 1)
                with dve.Fori(0, NB) as d:
                    lo, hi, skip = span(dve, d)
                    dve.wait_ge(nodes_ready, d + 1)
                    dve.wait_ge(hot_ready, lo * GA)
                    v.tensor_scalar(nodes_here[:], nodes_here[:], float(P), None, ALU.add).then_inc(nodes_ready, 1)
                    wait_alone(dve, (nodes_ready, d + 2))
                    with dve.Fori(lo, hi) as i:
                        for k in range(GA):
                            dve.wait_ge(summed[k], i)
                            v.tensor_scalar(hot[:, k, :], nodes_here[:], dst_f[:, bass.ds(tile_of(i, skip, k), 1)], None,
                                            ALU.is_equal).then_inc(hot_ready, 1)

            @block.tensor
            def _(pe):
                with pe.Fori(0, NB) as d:
                    lo, hi, skip = span(pe, d)
                    pe.wait_ge(s_kept, d)
                    nc.tensor.matmul(s_ps[:, 0:W0], zeros_bf[:, 0:P], zeros_bf[:, 0:W0], start=True, stop=False,
                                     skip_group_check=True)
                    with pe.Fori(lo, hi) as i:
                        for k in range(GA):
                            pe.wait_ge(x_in[k], i * 16 + 16)
                            pe.wait_ge(e_in[k], i * 16 + 16)
                            pe.wait_ge(hot_ready, i * GA + (k + 1))
                            nc.tensor.matmul(s_ps[:, 0:W0], hot[:, k, :], rows[:, k, :], start=False, stop=True,
                                             skip_group_check=True).then_inc(summed[k], 1)

        if debug == "aggregate":
            with nc.semaphore("dbg") as dbg, nc.Block() as block:
                @block.sync
                def _(sp):
                    sp.dma_start(a["o_s"], s_all[:]).then_inc(dbg, 16)
                    sp.wait_ge(dbg, 16)
            return

        with ExitStack() as ctx:
            w_edge = sb("w_edge", [P, D + 1], F32, ctx)
            b_parts = sb("b_parts", [P, D + 1], BF16, ctx)
            part_f = sb("part_f", [P, D + 1], F32, ctx)
            part_bf = sb("part_bf", [P, D + 1], BF16, ctx)
            ones_bf = sb("ones_bf", [P, P], BF16, ctx)
            row = {n: sb(f"row_{n}", [P, D], F32, ctx) for n in
                   ("a_tgt", "a_nbr", "a_edge", "w_b", "ew_b", "aggr_scale", "aggr_bias", "out_scale", "out_bias")}
            b_edge = sb("b_edge", [P, D + 1], F32, ctx)
            ab_col = sb("ab_col", [P, 1], F32, ctx)
            w_msg = sb("w_msg", [P, KC + 1, D], F32, ctx)
            w_mlp = sb("w_mlp", [P, 3, KC, D], F32, ctx)
            b_mlp = sb("b_mlp", [P, 3, KC], F32, ctx)
            w_node = sb("w_node", [P, KC, D], F32, ctx)
            junk = sb("junk", [P, D], F32, ctx)
            feats = sb("feats", [P, GA, P], F32, ctx)
            relu_y = sb("relu_y", [P, GA, D], F32, ctx)
            rec = [sb(f"rec{k}", [P, REC], I32, ctx) for k in range(GA)]
            x_blk = sb("x_blk", [P, D], F32, ctx)
            s_cur = sb("s_cur", [P, W0], F32, ctx)
            s_t = sb("s_t", [P, (KC + 1) * P], F32, ctx)
            u = sb("u", [P, D], F32, ctx)
            u2 = sb("u2", [P, D], F32, ctx)
            stats = sb("stats", [P, 6], F32, ctx)
            mv = sb("mv", [P, 2], F32, ctx)
            rstd = sb("rstd", [P, 1], F32, ctx)
            std = sb("std", [P, 1], F32, ctx)
            eps = [sb(f"eps{n}", [P, 1], F32, ctx) for n in range(3)]
            h_t = sb("h_t", [P, KC, P], F32, ctx)
            y_t = sb("y_t", [P, KC, P], F32, ctx)
            x1_cur = sb("x1_cur", [P, D], F32, ctx)
            x1_t = sb("x1_t", [P, KC, P], F32, ctx)
            tab = sb("tab", [P, HW], F32, ctx)
            p_cur = sb("p_cur", [P, 1], F32, ctx)

            w_in = sem("w_in", ctx)
            consts = sem("consts", ctx)
            dve_done = sem("dve_done2", ctx)
            f_in = [sem(f"f_in{k}", ctx) for k in range(GA)]
            y_ready = [sem(f"y_ready{k}", ctx) for k in range(GA)]
            relu_ready = [sem(f"relu_ready{k}", ctx) for k in range(GA)]
            rec_ready = [sem(f"rec_ready{k}", ctx) for k in range(GA)]
            logit_ready = [sem(f"logit_ready{k}", ctx) for k in range(GA)]
            rec_out = [sem(f"rec_out{k}", ctx) for k in range(GA)]
            nx = {n: sem("n_" + n, ctx) for n in (
                "x", "s", "sps", "st", "agg", "h0", "h0ps", "h0t", "y0", "y1", "y2", "act0", "act1", "act2",
                "res0", "res1", "res2", "back", "x1", "x1ps", "x1t", "hid", "tab", "tab_out", "dve", "p", "var", "std")}
            block = ctx.enter_context(nc.Block())
            STEPS = NT // GA
            assert PER >= 1
            TR, ND, YT, X1 = banks[4], banks[5], banks[6], banks[7]

            def parts(table, j, d):
                for n, fn in enumerate(table):
                    if min(n, PER - 1) == j:
                        fn(d)

            @block.sync
            def _(sp):
                def load(dst, src):
                    sp.dma_start(dst, src).then_inc(w_in, 16)

                load(w_edge[:, 0:D], a["ew_W"])
                for n, name in enumerate(("a_tgt", "a_nbr", "a_edge")):
                    load(row[name][:], a["a_W"][n:n + 1, :].to_broadcast([P, D]))
                for name in ("w_b", "ew_b", "aggr_scale", "aggr_bias", "out_scale", "out_bias"):
                    load(row[name][:], a[name].to_broadcast([P, D]))
                load(ab_col[:], a["a_b"].to_broadcast([P, 1]))
                for c in range(KC):
                    load(w_msg[:, c, :], a["W_message"][c * P:(c + 1) * P, :])
                    load(w_node[:, c, :], a["w_W"][c * P:(c + 1) * P, :])
                    for n in range(3):
                        load(w_mlp[:, n, c, :], a[f"mlp_W{n}"][c * P:(c + 1) * P, :])
                load(w_msg[0:DE0, KC, :], a["W_message"][D:D + DE0, :])
                for n in range(3):
                    load(b_mlp[:, n, :], a[f"mlp_b{n}"])

                def edge_step(i):
                    for k in range(GA):
                        sp.wait_ge(y_ready[k], i)
                        sp.dma_start(feats[:, k, :], a["edge128"][:, bass.ds((i * GA + k) * P, P)]).then_inc(f_in[k], 16)

                def load_x(d):
                    sp.wait_ge(nx["x1"], d)
                    sp.dma_start(x_blk[:], a["x"][bass.ds(d * P, P), :]).then_inc(nx["x"], 16)

                with sp.Fori(0, NB) as d:
                    for j in range(PER):
                        if j == 0:
                            load_x(d)
                        edge_step(d * PER + j)
                    sp.wait_ge(nx["tab"], d + 1)
                    sp.dma_start(nodetab[bass.ds(d * P, P), :], tab[:]).then_inc(nx["tab_out"], 16)
                with sp.Fori(NB * PER, STEPS) as i:
                    edge_step(i)
                sp.wait_ge(nx["tab_out"], NB * 16)

            W_LOADS = 1 + 3 + 6 + 1 + KC * 5 + 1 + 3

            @block.gpsimd
            def _(pool):
                with pool.Fori(0, STEPS) as i:
                    for k in range(GA):
                        wait_alone(pool, (logit_ready[k], i + 1))
                        pool.indirect_dma_start(
                            out=recs, out_offset=bass.IndirectOffsetOnAxis(ap=rec[k][:, 3:4].bitcast(U32), axis=0),
                            in_=rec[k][:], in_offset=None).then_inc(rec_out[k], 16)
                for k in range(GA):
                    pool.wait_ge(rec_out[k], STEPS * 16)

            @block.tensor
            def _(pe):
                pe.wait_ge(w_in, W_LOADS * 16)
                pe.wait_ge(consts, 1)
                mm = nc.tensor.matmul

                def edge_step(i):
                    for k in range(GA):
                        pe.wait_ge(f_in[k], i * 16 + 16)
                        pe.wait_ge(logit_ready[k], i)
                        mm(banks[k][:, 0:D + 1], feats[:, k, :], w_edge[:], start=True, stop=False)
                        mm(banks[k][:, 0:D + 1], ones_bf[0:3, :], b_parts[0:3, :], start=False, stop=True).then_inc(y_ready[k], 1)

                def turn_s(d):
                    pe.wait_ge(nx["s"], d + 1)
                    for c in range(KC):
                        nc.tensor.transpose(TR[:, c * P:(c + 1) * P], s_cur[:, c * P:(c + 1) * P], ident[:])
                    nc.tensor.transpose(TR[0:DE0, KC * P:(KC + 1) * P], s_cur[:, D:W0], ident[:]).then_inc(nx["sps"], 1)

                def messages(d):
                    pe.wait_ge(nx["st"], d + 1)
                    for c in range(KC):
                        mm(ND[:, 0:D], s_t[:, c * P:(c + 1) * P], w_msg[:, c, :], start=(c == 0), stop=False)
                    mm(ND[:, 0:D], s_t[0:DE0, KC * P:(KC + 1) * P], w_msg[0:DE0, KC, :], start=False,
                       stop=True).then_inc(nx["agg"], 1)

                def turn(out, src, done):
                    for c in range(KC):
                        ins = nc.tensor.transpose(out[:, c * P:(c + 1) * P], src(c), ident[:])
                    ins.then_inc(nx[done], 1)

                def layer(n, before):
                    def fn(d):
                        pe.wait_ge(nx[before], d + 1)
                        for m in range(KC):
                            for c in range(KC):
                                ins = mm(YT[:, m * P:(m + 1) * P], w_mlp[:, n, c, m * P:(m + 1) * P], h_t[:, c, :],
                                         start=(c == 0), stop=(c == KC - 1))
                        ins.then_inc(nx[f"y{n}"], 1)
                    return fn

                def first_layer(d):
                    pe.wait_ge(nx["h0"], d + 1)
                    turn(TR, lambda c: u[:, c * P:(c + 1) * P], "h0ps")
                    layer(0, "h0t")(d)

                def back(d):
                    pe.wait_ge(nx["res2"], d + 1)
                    turn(ND, lambda c: h_t[:, c, :], "back")

                def turn_x1(d):
                    pe.wait_ge(nx["x1"], d + 1)
                    turn(X1, lambda c: x1_cur[:, c * P:(c + 1) * P], "x1ps")

                def hidden(d):
                    pe.wait_ge(nx["x1t"], d + 1)
                    for c in range(KC):
                        ins = mm(ND[:, 0:D], x1_t[:, c, :], w_node[:, c, :], start=(c == 0), stop=(c == KC - 1))
                    ins.then_inc(nx["hid"], 1)

                node = [turn_s, messages, first_layer, layer(1, "res0"), layer(2, "res1"), back, turn_x1, hidden]
                with pe.Fori(0, NB) as d:
                    for j in range(PER):
                        edge_step(d * PER + j)
                        parts(node, j, d)
                with pe.Fori(NB * PER, STEPS) as i:
                    edge_step(i)

            @block.scalar
            def _(act):
                act.wait_ge(w_in, W_LOADS * 16)
                act.wait_ge(consts, 1)
                s = nc.scalar

                def edge_step(i):
                    for k in range(GA):
                        act.wait_ge(rec_out[k], i * 16)
                        s.copy(rec[k][:], place[:, bass.ds(i * GA + k, 1), :].squeeze(1)).then_inc(rec_ready[k], 1)
                        act.wait_ge(y_ready[k], i + 1)
                        s.activation(relu_y[:, k, :], banks[k][:, 0:D], ACT.Relu, scale=1.0 - SLOPE).then_inc(relu_ready[k], 1)

                def take_s(d):
                    act.wait_ge(nx["sps"], d)
                    s.copy(s_cur[:], s_all[:, bass.ds(d, 1), :].squeeze(1)).then_inc(nx["s"], 1)
                    act.wait_ge(nx["sps"], d + 1)
                    s.copy(s_t[:, 0:KC * P], TR[:, 0:KC * P])
                    s.copy(s_t[0:DE0, KC * P:(KC + 1) * P], TR[0:DE0, KC * P:(KC + 1) * P]).then_inc(nx["st"], 1)

                def take_h0(d):
                    act.wait_ge(nx["h0ps"], d + 1)
                    s.copy(h_t[:].rearrange("p c n -> p (c n)"), TR[:, 0:KC * P]).then_inc(nx["h0t"], 1)
                    layer(0)(d)

                def layer(n):
                    def fn(d):
                        act.wait_ge(nx[f"y{n}"], d + 1)
                        for m in range(KC):
                            ins = s.activation(y_t[:, m, :], YT[:, m * P:(m + 1) * P], ACT.Relu if n < 2 else ACT.Identity,
                                               bias=b_mlp[:, n, m:m + 1])
                        ins.then_inc(nx[f"act{n}"], 1)
                    return fn

                def take_x1(d):
                    act.wait_ge(nx["x1ps"], d + 1)
                    s.copy(x1_t[:].rearrange("p c n -> p (c n)"), X1[:, 0:KC * P]).then_inc(nx["x1t"], 1)
                    s.copy(x1_all[:, bass.ds(d, 1), :].squeeze(1), x1_cur[:]).then_inc(nx["p"], 1)

                def take_p(d):
                    act.wait_ge(nx["tab"], d + 1)
                    s.activation(p_all[:, bass.ds(d, 1)], p_cur[:], ACT.Identity, bias=ab_col[:, 0:1]).then_inc(nx["p"], 1)

                def deviation(*norms):
                    def fn(d):
                        for n in norms:
                            act.wait_ge(nx["var"], d * 3 + n + 1)
                            s.activation(std[:], mv[:, 1:2], ACT.Sqrt, bias=eps[n][:, 0:1]).then_inc(nx["std"], 1)
                    return fn

                skip = lambda d: None
                node = [take_s, deviation(0), take_h0, layer(1), layer(2), deviation(1, 2), take_x1, skip, take_p]
                with act.Fori(0, NB) as d:
                    for j in range(PER):
                        edge_step(d * PER + j)
                        parts(node, j, d)
                with act.Fori(NB * PER, STEPS) as i:
                    edge_step(i)
                act.wait_ge(nx["p"], 2 * NB)

            @block.vector
            def _(dve):
                v = nc.vector
                done = [0]

                def link(ins):
                    done[0] += 1
                    ins.then_inc(dve_done, 1)
                    dve.wait_ge(dve_done, done[0])

                dve.wait_ge(w_in, W_LOADS * 16)
                link(v.memset(ones_bf[:], 1.0))
                link(v.memset(tab[:], 1.0))
                for n, e in enumerate((LN_EPS, LN_EPS, RES_EPS)):
                    link(v.memset(eps[n][:], e))
                link(v.tensor_tensor_reduce(junk[:], w_edge[:, 0:D], row["a_edge"][:], 1.0, 0.0, ALU.mult, ALU.add,
                                            w_edge[:, D:D + 1]))
                link(v.tensor_copy(b_edge[:, 0:D], row["ew_b"][:]))
                link(v.tensor_tensor_reduce(junk[:], row["ew_b"][:], row["a_edge"][:], 1.0, 0.0, ALU.mult, ALU.add,
                                            b_edge[:, D:D + 1]))
                link(v.tensor_scalar(w_edge[:, D:D + 1], w_edge[:, D:D + 1], SLOPE, None, ALU.mult))
                link(v.tensor_scalar(b_edge[:, D:D + 1], b_edge[:, D:D + 1], SLOPE, None, ALU.mult))
                link(v.memset(b_parts[:], 0.0))
                for n in range(3):
                    link(v.tensor_copy(part_bf[:], b_edge[:]))
                    link(v.tensor_copy(part_f[:], part_bf[:]))
                    link(v.tensor_tensor(b_edge[:], b_edge[:], part_f[:], ALU.subtract))
                    link(v.tensor_scalar(rstd[:], lane[:, 0:1], float(n), None, ALU.is_equal))
                    link(v.scalar_tensor_tensor(b_parts[:], part_f[:], rstd[:, 0:1], b_parts[:], ALU.mult, ALU.add))
                v.memset(junk[:], 0.0).then_inc(consts, 1)

                def edge_step(i):
                    for k in range(GA):
                        dve.wait_ge(rec_ready[k], i + 1)
                        dve.wait_ge(relu_ready[k], i + 1)
                        v.tensor_tensor_reduce(relu_y[:, k, :], relu_y[:, k, :], row["a_edge"][:], 1.0, banks[k][:, D:D + 1],
                                               ALU.mult, ALU.add, rec[k][:, 2:3].bitcast(F32)).then_inc(logit_ready[k], 1)

                NDV = 18
                count = [0]

                def step(d, ins):
                    count[0] += 1
                    ins.then_inc(nx["dve"], 1)
                    wait_alone(dve, (nx["dve"], d * NDV + count[0]))

                def normed(d, n, out, src):
                    step(d, v.bn_stats(stats[:], src))
                    v.bn_aggr(mv[:], stats[:]).then_inc(nx["var"], 1)
                    dve.wait_ge(nx["std"], d * 3 + n + 1)
                    step(d, v.reciprocal(rstd[:], std[:]))
                    return v.tensor_scalar(out, src, mv[:, 0:1], rstd[:, 0:1], ALU.subtract, ALU.mult)

                def first_norm(d):
                    dve.wait_ge(nx["agg"], d + 1)
                    dve.wait_ge(nx["x"], d * 16 + 16)
                    step(d, v.scalar_tensor_tensor(u2[:], ND[:, 0:D], 0.0, x_blk[:], ALU.max, ALU.add))
                    step(d, normed(d, 0, u2[:], u2[:]))
                    step(d, v.tensor_tensor(u2[:], u2[:], row["aggr_scale"][:], ALU.mult))
                    v.tensor_tensor(u[:], u2[:], row["aggr_bias"][:], ALU.add).then_inc(nx["h0"], 1)

                def residual(n):
                    def fn(d):
                        dve.wait_ge(nx[f"act{n}"], d + 1)
                        v.tensor_tensor(h_t[:], h_t[:], y_t[:], ALU.add).then_inc(nx[f"res{n}"], 1)
                    return fn

                def out_norms(d):
                    dve.wait_ge(nx["back"], d + 1)
                    step(d, v.tensor_tensor(u2[:], ND[:, 0:D], x_blk[:], ALU.add))
                    step(d, normed(d, 1, u2[:], u2[:]))
                    step(d, v.tensor_tensor(u2[:], u2[:], row["out_scale"][:], ALU.mult))
                    step(d, v.tensor_tensor(u2[:], u2[:], row["out_bias"][:], ALU.add))
                    step(d, v.tensor_tensor(u2[:], u2[:], x_blk[:], ALU.add))
                    dve.wait_ge(nx["p"], d * 2)
                    normed(d, 2, x1_cur[:], u2[:]).then_inc(nx["x1"], 1)

                def table(d):
                    dve.wait_ge(nx["hid"], d + 1)
                    dve.wait_ge(nx["tab_out"], d * 16)
                    step(d, v.tensor_tensor(u2[:], ND[:, 0:D], row["w_b"][:], ALU.add))
                    step(d, v.scalar_tensor_tensor(tab[:, 0:D], u2[:], SLOPE, u2[:], ALU.mult, ALU.max))
                    step(d, v.tensor_tensor_reduce(u2[:], tab[:, 0:D], row["a_nbr"][:], 1.0, 0.0, ALU.mult, ALU.add,
                                                   tab[:, D:D + 1]))
                    step(d, v.tensor_tensor_reduce(u2[:], tab[:, 0:D], row["a_tgt"][:], 1.0, 0.0, ALU.mult, ALU.add,
                                                   p_cur[:]))
                    v.memset(stats[:], 0.0).then_inc(nx["tab"], 1)
                    assert count[0] == NDV, count[0]

                skip = lambda d: None
                node = [skip, first_norm, residual(0), residual(1), residual(2), out_norms, skip, table]
                with dve.Fori(0, NB) as d:
                    for j in range(PER):
                        edge_step(d * PER + j)
                        parts(node, j, d)
                with dve.Fori(NB * PER, STEPS) as i:
                    edge_step(i)

        if debug == "edges":
            with nc.semaphore("dbg") as dbg, nc.Block() as block:
                @block.sync
                def _(sp):
                    sp.dma_start(a["o_x1"], x1_all[:]).then_inc(dbg, 16)
                    sp.dma_start(a["o_p"], p_all[:]).then_inc(dbg, 16)
                    sp.dma_start(a["o_tab"], nodetab).then_inc(dbg, 16)
                    sp.dma_start(a["o_recs"], recs).then_inc(dbg, 16)
                    sp.dma_start(a["o_place"], place[:]).then_inc(dbg, 16)
                    sp.wait_ge(dbg, 5*16)
            return
        mid.close()

        o_all = sb("o_all", [P, NB, HW])
        HALF = GC // 2
        with ExitStack() as ctx:
            recs_sb = sb("recs_sb", [P, RT, REC], I32, ctx)
            lane_f = sb("lane_f", [P, RT], F32, ctx)
            nbr_all = sb("nbr_all", [P, RT], I32, ctx)
            nbr = sb("nbr", [P, GC, HW], F32, ctx)
            nbr_idx = [sb(f"nbr_idx{f}", [P, HALF], I32, ctx) for f in range(2)]
            logit = [sb(f"logit{f}", [P, HALF], F32, ctx) for f in range(2)]
            w = sb("w", [P, GC, P], F32, ctx)
            p_row = sb("p_row", [P, P], F32, ctx)
            p_diag = sb("p_diag", [P, P], F32, ctx)
            m_diag = [sb(f"m_diag{f}", [P, P], F32, ctx) for f in range(2)]
            top_new = sb("top_new", [P, 1], F32, ctx)
            m = [sb(f"m{f}", [P, 1], F32, ctx) for f in range(2)]
            fall = [sb(f"fall{f}", [P, 1], F32, ctx) for f in range(2)]
            decay = [sb(f"decay{f}", [P, 1], F32, ctx) for f in range(2)]
            acc = sb("acc", [P, HW], F32, ctx)
            T_PS, M_PS, O_PS, P_PS = banks[0:2], banks[2:4], banks[4:6], banks[6]

            recs_in = sem("recs_in", ctx)
            lanes_ready = sem("lanes_ready", ctx)
            idx_in = [sem(f"idx_in{f}", ctx) for f in range(2)]
            nbr_in = [sem(f"nbr_in{k}", ctx) for k in range(GC)]
            used = [sem(f"used{k}", ctx) for k in range(GC)]
            p_diag_ready = sem("p_diag_ready", ctx)
            p_row_ps = sem("p_row_ps", ctx)
            p_row_ready = sem("p_row_ready", ctx)
            x_ready = sem("x_ready", ctx)
            turned = [sem(f"turned{f}", ctx) for f in range(2)]
            fall_ready = [sem(f"fall_ready{f}", ctx) for f in range(2)]
            decay_ready = [sem(f"decay_ready{f}", ctx) for f in range(2)]
            m_diag_ready = [sem(f"m_diag_ready{f}", ctx) for f in range(2)]
            m_row = [sem(f"m_row{f}", ctx) for f in range(2)]
            y_ready = [sem(f"yc_ready{f}", ctx) for f in range(2)]
            w_ready = [sem(f"w_ready{f}", ctx) for f in range(2)]
            added = [sem(f"added{f}", ctx) for f in range(2)]
            acc_kept = sem("acc_kept", ctx)
            dve_step = sem("dve_step", ctx)
            max_ready = [sem(f"max_ready{f}", ctx) for f in range(2)]
            reset = sem("reset", ctx)
            block = ctx.enter_context(nc.Block())

            def span(eng, d):
                col = bass.ds(d, 1)
                lo = eng.value_load(c_start[0:1, col], min_val=0, max_val=RT // GC - 1)
                hi = eng.value_load(c_end[0:1, col], min_val=1, max_val=RT // GC)
                return lo, hi

            def tile0(i):
                return i.with_bounds(min_val=0, max_val=RT // GC - 1) * GC

            @block.sync
            def _(sp):
                sp.dma_start(recs_sb[:], recs_pt).then_inc(recs_in, 16)
                sp.wait_ge(lanes_ready, 2)
                with sp.Fori(0, NB) as d:
                    lo, hi = span(sp, d)
                    with sp.Fori(lo, hi) as i:
                        for f in range(2):
                            for k in range(HALF):
                                sp.wait_ge(nbr_in[f * HALF + k], i * 16)
                            sp.dma_start(nbr_idx[f][:], nbr_all[:, bass.ds(tile0(i) + f * HALF, HALF)]).then_inc(idx_in[f], 16)

            @block.gpsimd
            def _(pool):
                with pool.Fori(0, NB) as d:
                    lo, hi = span(pool, d)
                    with pool.Fori(lo, hi) as i:
                        for k in range(GC):
                            wait_alone(pool, (idx_in[k // HALF], i * 16 + 16), (used[k], i))
                            pool.indirect_dma_start(
                                out=nbr[:, k, :], out_offset=None, in_=nodetab,
                                in_offset=bass.IndirectOffsetOnAxis(
                                    ap=nbr_idx[k // HALF][:, k % HALF:k % HALF + 1].bitcast(U32), axis=0),
                            ).then_inc(nbr_in[k], 16)

            @block.tensor
            def _(pe):
                mm = nc.tensor.matmul
                with pe.Fori(0, NB) as d:
                    lo, hi = span(pe, d)
                    pe.wait_ge(p_diag_ready, d + 1)
                    mm(P_PS[:, 0:P], ones[:], p_diag[:], start=True, stop=True).then_inc(p_row_ps, 1)
                    with pe.Fori(lo, hi) as i:
                        for f in range(2):
                            pe.wait_ge(x_ready, i * GC + (f + 1) * HALF)
                            pe.wait_ge(fall_ready[f], i)
                            for k in range(HALF):
                                ins = nc.tensor.transpose(T_PS[f][:, k * P:(k + 1) * P], w[:, f * HALF + k, :], ident[:])
                            ins.then_inc(turned[f], 1)
                            pe.wait_ge(m_diag_ready[f], i + 1)
                            mm(M_PS[f][:, 0:P], ones[:], m_diag[f][:], start=True, stop=True).then_inc(m_row[f], 1)
                        for f in range(2):
                            pe.wait_ge(w_ready[f], i + 1)
                            pe.wait_ge(added[f], i)
                            for k in range(HALF):
                                mm(O_PS[f][:, 0:HW], w[:, f * HALF + k, :], nbr[:, f * HALF + k, :], start=(k == 0),
                                   stop=(k == HALF - 1)).then_inc(used[f * HALF + k], 1)

            @block.scalar
            def _(act):
                s = nc.scalar
                with act.Fori(0, NB) as d:
                    lo, hi = span(act, d)
                    act.wait_ge(p_row_ps, d + 1)
                    act.wait_ge(x_ready, lo * GC)
                    s.copy(p_row[:], P_PS[:, 0:P]).then_inc(p_row_ready, 1)
                    with act.Fori(lo, hi) as i:
                        for f in range(2):
                            act.wait_ge(fall_ready[f], i + 1)
                            act.wait_ge(added[f], i)
                            s.activation(decay[f][:], fall[f][:], ACT.Exp).then_inc(decay_ready[f], 1)
                            act.wait_ge(y_ready[f], i + 1)
                            half = w[:, f * HALF:(f + 1) * HALF, :]
                            s.activation(half, half, ACT.Exp).then_inc(w_ready[f], 1)
                    act.wait_ge(added[1], hi)
                    s.copy(o_all[:, bass.ds(d, 1), :].squeeze(1), acc[:]).then_inc(acc_kept, 1)

            @block.vector
            def _(dve):
                v = nc.vector
                dve.wait_ge(recs_in, 16)
                v.tensor_copy(lane_f[:], recs_sb[:, :, 0]).then_inc(lanes_ready, 1)
                v.tensor_copy(nbr_all[:], recs_sb[:, :, 1]).then_inc(lanes_ready, 1)
                dve.wait_ge(lanes_ready, 2)
                NDV = 2 * (HALF + 2)
                count = [0]

                def step(i, ins):
                    count[0] += 1
                    ins.then_inc(dve_step, 1)
                    dve.wait_ge(dve_step, i * NDV + count[0])

                def logits(i, f):
                    for k in range(f * HALF, (f + 1) * HALF):
                        dve.wait_ge(used[k], i)
                        ins = v.tensor_scalar(w[:, k, :], iota[:], lane_f[:, bass.ds(tile0(i) + k, 1)], MASKED,
                                              ALU.not_equal, ALU.mult)
                        if k < (f + 1) * HALF - 1:
                            ins.then_inc(dve_step, 1)
                            count[0] += 1
                    step(i, ins)
                    for k in range(f * HALF, (f + 1) * HALF):
                        dve.wait_ge(nbr_in[k], i * 16 + 16)
                    step(i, v.tensor_tensor(logit[f][:], recs_sb[:, bass.ds(tile0(i) + f * HALF, HALF), 2].bitcast(F32),
                                            nbr[:, f * HALF:(f + 1) * HALF, D], ALU.add))
                    for k in range(HALF):
                        v.scalar_tensor_tensor(w[:, f * HALF + k, :], w[:, f * HALF + k, :], logit[f][:, k:k + 1], p_row[:],
                                               ALU.add, ALU.add).then_inc(x_ready, 1)

                def maximum(i, f):
                    dve.wait_ge(turned[f], i + 1)
                    step(i, v.tensor_reduce(top_new[:], T_PS[f][:, :], AX.X, ALU.max))
                    other = m[1 - f]
                    dve.wait_ge(decay_ready[f], i)
                    v.tensor_tensor(other[:], top_new[:], m[f][:], ALU.max).then_inc(max_ready[f], 1)
                    dve.wait_ge(max_ready[f], i + 1)
                    v.tensor_tensor(fall[f][:], m[f][:], other[:], ALU.subtract).then_inc(fall_ready[f], 1)
                    v.tensor_scalar(m_diag[f][:], ident[:], other[:, 0:1], None, ALU.mult).then_inc(m_diag_ready[f], 1)

                def below_maximum(i, f):
                    dve.wait_ge(m_row[f], i + 1)
                    half = w[:, f * HALF:(f + 1) * HALF, :]
                    v.tensor_tensor(half, half, M_PS[f][:, 0:P].unsqueeze(1).to_broadcast([P, HALF, P]),
                                    ALU.subtract).then_inc(y_ready[f], 1)

                def add(i, f):
                    dve.wait_ge(used[f * HALF + HALF - 1], i + 1)
                    dve.wait_ge(decay_ready[f], i + 1)
                    if f:
                        dve.wait_ge(added[0], i + 1)
                    else:
                        dve.wait_ge(added[1], i)
                    v.scalar_tensor_tensor(acc[:], acc[:], decay[f][:, 0:1], O_PS[f][:, 0:HW], ALU.mult,
                                           ALU.add).then_inc(added[f], 1)

                with dve.Fori(0, NB) as d:
                    lo, hi = span(dve, d)
                    dve.wait_ge(acc_kept, d)
                    dve.wait_ge(p_row_ps, d)
                    v.memset(m[0][:], LOWEST).then_inc(reset, 1)
                    v.memset(acc[:], 0.0).then_inc(reset, 1)
                    v.tensor_scalar(p_diag[:], ident[:], p_all[:, bass.ds(d, 1)], None, ALU.mult).then_inc(p_diag_ready, 1)
                    wait_alone(dve, (p_row_ready, d + 1), (reset, d * 2 + 2))
                    with dve.Fori(lo, hi) as i:
                        count[0] = 0
                        logits(i, 0)
                        maximum(i, 0)
                        logits(i, 1)
                        below_maximum(i, 0)
                        maximum(i, 1)
                        below_maximum(i, 1)
                        add(i, 0)
                        add(i, 1)
                        assert count[0] == NDV, count[0]

        with ExitStack() as ctx:
            den = sb("den", [P, 1], F32, ctx)
            inv = sb("inv", [P, 1], F32, ctx)
            y = sb("y", [P, D], F32, ctx)
            y2 = sb("y2", [P, D], F32, ctx)
            res = [sb(f"res{b}", [P, D], F32, ctx) for b in range(2)]
            stats = sb("stats_f", [P, 6], F32, ctx)
            mv = sb("mv_f", [P, 2], F32, ctx)
            std = sb("std_f", [P, 1], F32, ctx)
            eps = sb("eps_f", [P, 1], F32, ctx)
            var_ready = sem("var_ready", ctx)
            std_ready = sem("std_ready", ctx)
            eps_ready = sem("eps_ready", ctx)
            res_ready = sem("res_ready", ctx)
            out_done = sem("out_done", ctx)
            step_done = sem("step_done", ctx)
            block = ctx.enter_context(nc.Block())
            LAST = n_nodes - (NB - 1) * P

            @block.sync
            def _(sp):
                with sp.Fori(0, NB - 1) as d:
                    sp.wait_ge(res_ready, d + 1)
                    sp.dma_start(a["out"][bass.ds(d * P, P), :], res[0][:]).then_inc(out_done, 16)
                sp.wait_ge(res_ready, NB)
                sp.dma_start(a["out"][(NB - 1) * P:n_nodes, :], res[0][0:LAST, :]).then_inc(out_done, 16)
                sp.wait_ge(out_done, NB * 16)

            @block.scalar
            def _(act):
                act.wait_ge(eps_ready, 1)
                with act.Fori(0, NB) as d:
                    act.wait_ge(var_ready, d + 1)
                    nc.scalar.activation(std[:], mv[:, 1:2], ACT.Sqrt, bias=eps[:, 0:1]).then_inc(std_ready, 1)

            @block.vector
            def _(dve):
                v = nc.vector
                v.memset(eps[:], RES_EPS).then_inc(eps_ready, 1)
                NDV = 7
                with dve.Fori(0, NB) as d:
                    count = [0]

                    def step(ins):
                        count[0] += 1
                        ins.then_inc(step_done, 1)
                        wait_alone(dve, (step_done, d * NDV + count[0]))

                    row_d = bass.ds(d, 1)
                    step(v.tensor_scalar(den[:], o_all[:, row_d, D + 1], 1e-30, None, ALU.max))
                    step(v.reciprocal(inv[:], den[:]))
                    step(v.tensor_scalar(y[:], o_all[:, row_d, 0:D].squeeze(1), inv[:, 0:1], None, ALU.mult))
                    step(v.scalar_tensor_tensor(y2[:], y[:], SLOPE, y[:], ALU.mult, ALU.max))
                    step(v.tensor_tensor(y[:], y2[:], x1_all[:, row_d, :].squeeze(1), ALU.add))
                    step(v.bn_stats(stats[:], y[:]))
                    v.bn_aggr(mv[:], stats[:]).then_inc(var_ready, 1)
                    dve.wait_ge(std_ready, d + 1)
                    step(v.reciprocal(inv[:], std[:]))
                    dve.wait_ge(out_done, d * 16)
                    v.tensor_scalar(res[0][:], y[:], mv[:, 0:1], inv[:, 0:1], ALU.subtract, ALU.mult).then_inc(res_ready, 1)
                    assert count[0] == NDV, count[0]


def layout(f):
    import numpy as np

    f = {k: np.asarray(v) for k, v in f.items()}
    n_nodes, n_edges = f["x"].shape[0], f["src"].shape[0]
    z = sizes(n_nodes, n_edges)
    none = z["blocks"] * P
    more = z["tiles"] * P - n_edges

    def lanes(v):
        return np.ascontiguousarray(np.pad(v, (0, more), constant_values=none).reshape(-1, P).T)

    groups = np.pad(f["dst"], (0, z["gp"] * P * GA * P - n_edges), constant_values=none)
    e64 = np.pad(f["edge_attr_64"], ((0, more), (0, 0)))
    ins = dict(
        x=np.pad(f["x"], ((0, none + P - n_nodes), (0, 0))),
        src=lanes(f["src"]),
        dst=lanes(f["dst"]),
        dst_groups=groups.reshape(P, z["gp"], GA * P),
        edge64=np.ascontiguousarray(e64.reshape(z["tiles"], P, -1).transpose(1, 0, 2)),
        edge128=np.ascontiguousarray(np.pad(f["edge_attr_128"], ((0, more), (0, 0))).T),
        W_message=f["L0_gnn_W_message"],
        a_W=f["L1_gnn_a_W"].reshape(3, -1),
        a_b=f["L1_gnn_a_b"].reshape(1, 1),
        w_W=f["L1_gnn_w_W"],
        ew_W=f["L1_gnn_ew_W"],
        w_b=f["L1_gnn_w_b"].reshape(1, -1),
        ew_b=f["L1_gnn_ew_b"].reshape(1, -1),
    )
    for n in range(3):
        ins[f"mlp_W{n}"] = f[f"L0_gnn_mlp_W{n}"]
        ins[f"mlp_b{n}"] = np.ascontiguousarray(f[f"L0_gnn_mlp_b{n}"].reshape(-1, P).T)
    for n in ("aggr_scale", "aggr_bias", "out_scale", "out_bias"):
        ins[n] = f[f"L0_gnn_ln_{n}"].reshape(1, -1)
    return ins


def kernel(**inputs):
    import numpy as np
    import concourse.bacc as bacc
    from concourse.bass_utils import run_bass_kernel_spmd

    n_nodes, n_edges = inputs["x"].shape[0], inputs["src"].shape[0]
    arrays = {k: np.ascontiguousarray(v) for k, v in layout(inputs).items()}
    nc = bacc.Bacc("TRN2", target_bir_lowering=False, num_devices=1)
    a = {k: nc.dram_tensor(f"in_{k}", v.shape, mybir.dt.from_np(v.dtype), kind="ExternalInput").ap()
         for k, v in arrays.items()}
    a["out"] = nc.dram_tensor("out", inputs["x"].shape, F32, kind="ExternalOutput").ap()
    build(nc, a, n_nodes, n_edges)
    r = run_bass_kernel_spmd(nc, [{f"in_{k}": v for k, v in arrays.items()}], core_ids=[0])
    return r.results[0]["out"]
```

```python
from contextlib import ExitStack

import concourse.bass as bass
from concourse import mybir

ALU = mybir.AluOpType
ACT = mybir.ActivationFunctionType
F32 = mybir.dt.float32
BF16 = mybir.dt.bfloat16
I32 = mybir.dt.int32
U32 = mybir.dt.uint32
U16 = mybir.dt.uint16
AX = mybir.AxisListType

P = 128
GA = 4
GC = 4
TURN = 4
GR = 2 * GA
SLOPE = 0.2
LN_EPS = 1e-6
RES_EPS = 1e-5
MASKED = -1e38
LOWEST = -1e37
REC = 4


def sizes(n_nodes, n_edges):
    tiles = -(-n_edges // P)
    tiles = -(-tiles // GR) * GR
    blocks = -(-n_nodes // P)
    groups = tiles // GA
    buckets = blocks + 1
    bucket_groups = -(-(tiles // GC + buckets + TURN) // (2 * TURN)) * 2 * TURN
    return dict(tiles=tiles, blocks=blocks, groups=groups, gp=-(-groups // P), rec_tiles=bucket_groups * GC)


def build(nc, a, n_nodes, n_edges):
    z = sizes(n_nodes, n_edges)
    NT, NB, NG, GP, RT = z["tiles"], z["blocks"], z["groups"], z["gp"], z["rec_tiles"]
    NH = NB + 1
    D = a["x"].shape[1]
    DE0 = a["edge64"].shape[2]
    W0 = D + DE0
    KC = D // P
    HW = D + 2
    PER = NT // GR // NB * 2
    NGC = RT // GC
    FAR = 4096.0

    nodetab = nc.dram_tensor("nodetab", [NB * P, HW], F32, kind="Internal").ap()
    recs = nc.dram_tensor("recs", [P * RT, REC], I32, kind="Internal").ap()
    recs_pt = recs.rearrange("(p t) w -> p t w", t=RT)

    with ExitStack() as top:
        def sb(name, shape, dt=F32, ctx=top):
            return ctx.enter_context(nc.sbuf_tensor(name, shape, dt))

        def sem(name, ctx=top):
            return ctx.enter_context(nc.semaphore(name))

        banks = [top.enter_context(nc.psum_tensor(f"bank{i}", [P, 512], F32)) for i in range(8)]

        opened = sem("opened")

        def wait_alone(eng, *waits):
            waits = [(on, eng.to_reg(count)) for on, count in waits]
            eng.wait_ge(opened, 1)
            for on, count in waits:
                eng.wait_ge(on, count)

        iota = sb("iota", [P, P])
        lane = sb("lane", [P, 1])
        ident = sb("ident", [P, P])
        ones = sb("ones", [P, P])
        zeros_bf = sb("zeros_bf", [P, 512], BF16)
        a_start = sb("a_start", [P, NB], I32)
        a_end = sb("a_end", [P, NB], I32)
        a_skip = sb("a_skip", [P, NB], I32)
        c_turns = sb("c_turns", [P, 2], I32)
        c_block = sb("c_block", [P, NGC], I32)
        p_all = sb("p_all", [P, NH])
        x1_all = sb("x1_all", [P, NB, D])

        mid = top.enter_context(ExitStack())
        dst_f = sb("dst_f", [P, NT], F32, mid)
        src_i = sb("src_i", [P, NT], I32, mid)
        place = sb("place", [P, NT, REC], I32, mid)
        s_all = sb("s_all", [P, NB, W0], F32, mid)

        with ExitStack() as ctx:
            dst_i = sb("dst_i", [P, NT], I32, ctx)
            hi_i = sb("hi_i", [P, NT], I32, ctx)
            hi_bf = sb("hi_bf", [P, NT], BF16, ctx)
            same = sb("same", [P, NT], BF16, ctx)
            rank_h = sb("rank_h", [P, NT], F32, ctx)
            rank = sb("rank", [P, NT], F32, ctx)
            tot = sb("tot", [P, NH], F32, ctx)
            first = sb("first", [P, NH], F32, ctx)
            dst_g = sb("dst_g", [P, GP, GA * P], I32, ctx)
            gmin = sb("gmin", [P, GP], F32, ctx)
            gmax = sb("gmax", [P, GP], F32, ctx)
            blk_i = sb("blk_i", [P, GP], I32, ctx)
            gnum = sb("gnum", [P, GP], F32, ctx)
            gnum_i = sb("gnum_i", [P, GP], I32, ctx)
            iota_h = sb("iota_h", [P, NH], F32, ctx)
            iota_i = sb("iota_i", [P, P], I32, ctx)
            lane_i = sb("lane_i", [P, 1], I32, ctx)
            below = sb("below", [P, P], F32, ctx)
            le = sb("le", [P, NB, GP], F32, ctx)
            ge = sb("ge", [P, NB, GP], F32, ctx)
            cand = sb("cand", [P, 2, NB], F32, ctx)
            best = sb("best", [P, 2, NB], F32, ctx)
            lo = sb("lo", [P, NB], F32, ctx)
            cnt = sb("cnt", [P, NH], F32, ctx)
            cnt_i = sb("cnt_i", [P, NH], I32, ctx)
            cum = sb("cum", [P, NH], F32, ctx)
            zrow = sb("zrow", [P, NH], F32, ctx)
            diag = sb("diag", [P, NH], F32, ctx)
            end_col = sb("end_col", [P, 1], F32, ctx)
            turns_i = sb("turns_i", [P, 1], I32, ctx)
            gnum_c = sb("gnum_c", [P, NGC], F32, ctx)
            gnum_ci = sb("gnum_ci", [P, NGC], I32, ctx)
            past = sb("past", [P, NGC], F32, ctx)
            blank = sb("blank", [P, RT // 8, REC], I32, ctx)
            idx_in = sem("idx_in", ctx)
            iota_done = sem("iota_done", ctx)
            dve_done = sem("dve_done", ctx)
            blank_ready = sem("blank_ready", ctx)
            blanked = sem("blanked", ctx)
            cand_ready = sem("cand_ready", ctx)
            best_ready = sem("best_ready", ctx)
            counts_ready = sem("counts_ready", ctx)
            sums_ready = sem("sums_ready", ctx)
            block = ctx.enter_context(nc.Block())

            @block.sync
            def _(sp):
                sp.dma_start(dst_g[:], a["dst_groups"]).then_inc(idx_in, 16)
                sp.dma_start(dst_i[:], a["dst"]).then_inc(idx_in, 16)
                sp.dma_start(src_i[:], a["src"]).then_inc(idx_in, 16)
                sp.wait_ge(blank_ready, 1)
                for j in range(8):
                    sp.dma_start(recs_pt[:, j * (RT // 8):(j + 1) * (RT // 8), :], blank[:]).then_inc(blanked, 16)
                sp.wait_ge(blanked, 8 * 16)

            @block.gpsimd
            def _(pool):
                nc.gpsimd.iota(iota_i[:], pattern=[[1, P]], base=0, channel_multiplier=0).then_inc(iota_done, 1)
                nc.gpsimd.iota(lane_i[:], pattern=[[1, 1]], base=0, channel_multiplier=1).then_inc(iota_done, 1)
                nc.gpsimd.iota(gnum_i[:], pattern=[[1, GP]], base=0, channel_multiplier=GP).then_inc(iota_done, 1)
                nc.gpsimd.iota(gnum_ci[:], pattern=[[1, NGC]], base=0, channel_multiplier=0).then_inc(iota_done, 1)
                pool.wait_ge(cand_ready, 1)
                nc.gpsimd.partition_all_reduce(best[:].rearrange("p a b -> p (a b)"), cand[:].rearrange("p a b -> p (a b)"),
                                               P, bass.bass_isa.ReduceOp.max).then_inc(best_ready, 1)

            @block.tensor
            def _(pe):
                pe.wait_ge(counts_ready, 1)
                nc.tensor.matmul(banks[0][:, 0:NH], below[:], tot[:], start=True, stop=True)
                nc.tensor.matmul(banks[1][:, 0:NH], ones[:], tot[:], start=True, stop=True).then_inc(sums_ready, 1)
                pe.wait_ge(counts_ready, 2)
                nc.tensor.matmul(banks[2][:, 0:NGC], ones[0:NB, :], past[0:NB, :], start=True, stop=True).then_inc(sums_ready, 1)

            @block.vector
            def _(dve):
                done = [0]

                def link(ins):
                    done[0] += 1
                    ins.then_inc(dve_done, 1)
                    dve.wait_ge(dve_done, done[0])

                v = nc.vector
                link(v.memset(blank[:], 0))
                v.memset(blank[:, :, 0:1], 2 * P).then_inc(blank_ready, 1)
                v.memset(zrow[:], 0.0).then_inc(opened, 1)
                dve.wait_ge(opened, 1)
                link(v.memset(ones[:], 1.0))
                link(v.memset(zeros_bf[:], 0.0))
                link(v.memset(zrow[:], 0.0))
                link(v.memset(place[:], 0))
                link(v.memset(rank[:], 1.0))
                dve.wait_ge(iota_done, 4)
                link(v.tensor_copy(iota[:], iota_i[:]))
                link(v.tensor_copy(lane[:], lane_i[:]))
                link(v.tensor_copy(gnum[:], gnum_i[:]))
                link(v.tensor_copy(iota_h[:], iota_i[:, 0:NH]))
                link(v.tensor_scalar(ident[:], iota[:], lane[:, 0:1], None, ALU.is_equal))
                link(v.tensor_scalar(below[:], iota[:], lane[:, 0:1], None, ALU.is_gt))

                dve.wait_ge(idx_in, 3 * 16)
                link(v.tensor_reduce(gmin[:], dst_g[:], AX.X, ALU.min))
                link(v.tensor_reduce(gmax[:], dst_g[:], AX.X, ALU.max))
                for g in (gmin, gmax):
                    link(v.tensor_copy(blk_i[:], g[:]))
                    link(v.tensor_scalar(blk_i[:], blk_i[:], 7, None, ALU.logical_shift_right))
                    link(v.tensor_copy(g[:], blk_i[:]))

                def over_blocks(t):
                    return t.unsqueeze(1).to_broadcast([P, NB, GP])

                d_all = iota_h[:, 0:NB].unsqueeze(2).to_broadcast([P, NB, GP])
                link(v.tensor_tensor(le[:], over_blocks(gmin[:]), d_all, ALU.is_le))
                link(v.tensor_tensor(ge[:], over_blocks(gmax[:]), d_all, ALU.is_ge))
                link(v.tensor_tensor(le[:], le[:], ge[:], ALU.mult))
                link(v.tensor_scalar(gmin[:], gnum[:], 1.0, None, ALU.add))
                link(v.tensor_scalar(gmax[:], gnum[:], -1.0, FAR, ALU.mult, ALU.add))
                link(v.tensor_tensor(ge[:], le[:], over_blocks(gmin[:]), ALU.mult))
                link(v.tensor_reduce(cand[:, 0, :], ge[:], AX.X, ALU.max))
                link(v.tensor_tensor(ge[:], le[:], over_blocks(gmax[:]), ALU.mult))
                link(v.tensor_reduce(cand[:, 1, :], ge[:], AX.X, ALU.max))
                v.memset(lo[:], 0.0).then_inc(cand_ready, 1)
                dve.wait_ge(best_ready, 1)
                link(v.tensor_scalar(lo[:], best[:, 1, :], -1.0, FAR, ALU.mult, ALU.add))
                link(v.tensor_scalar(lo[:], lo[:], float(NG - 1), None, ALU.min))
                link(v.tensor_tensor(cnt[:, 0:NB], best[:, 0, :], lo[:], ALU.subtract))
                link(v.tensor_scalar(cnt[:, 0:NB], cnt[:, 0:NB], 1.0, None, ALU.max))
                link(v.tensor_tensor_scan(cum[:, 0:NB], cnt[:, 0:NB], zrow[:, 0:NB], 0.0, ALU.add, ALU.add))
                link(v.tensor_copy(a_end[:], cum[:, 0:NB]))
                link(v.tensor_tensor(cum[:, 0:NB], cum[:, 0:NB], cnt[:, 0:NB], ALU.subtract))
                link(v.tensor_copy(a_start[:], cum[:, 0:NB]))
                link(v.tensor_tensor(lo[:], lo[:], cum[:, 0:NB], ALU.subtract))
                link(v.tensor_scalar(a_skip[:], lo[:], FAR, None, ALU.add))

                link(v.tensor_copy(dst_f[:], dst_i[:]))
                link(v.tensor_scalar(place[:, :, 1], dst_f[:], float(NB * P - 1), None, ALU.min))
                v.memset(p_all[:], 0.0).then_inc(dve_done, 1)
                done[0] += 1
                link(v.tensor_scalar(hi_i[:], src_i[:], 7, None, ALU.logical_shift_right))
                link(v.tensor_scalar(place[:, :, 0], src_i[:], P - 1, None, ALU.bitwise_and))
                link(v.tensor_copy(hi_bf[:], hi_i[:]))

                base = done[0]
                with dve.Fori(0, NH) as h:
                    v.tensor_scalar(same[:], hi_bf[:], iota_h[:, bass.ds(h, 1)], None, ALU.is_equal).then_inc(dve_done, 1)
                    dve.wait_ge(dve_done, h * 2 + (base + 1))
                    v.tensor_reduce(tot[:, bass.ds(h, 1)], same[:], AX.X, ALU.add).then_inc(dve_done, 1)
                    dve.wait_ge(dve_done, h * 2 + (base + 2))
                done[0] = base + 2 * NH
                v.memset(cnt[:], 0.0).then_inc(counts_ready, 1)
                dve.wait_ge(sums_ready, 1)
                link(v.tensor_scalar(cnt[:], banks[1][:, 0:NH], float(GC * P - 1), None, ALU.add))
                link(v.tensor_copy(cnt_i[:], cnt[:]))
                shift = (GC * P).bit_length() - 1
                link(v.tensor_scalar(cnt_i[:], cnt_i[:], shift, None, ALU.logical_shift_right))
                link(v.tensor_copy(cnt[:], cnt_i[:]))
                link(v.tensor_scalar(cnt[:], cnt[:], 1.0, None, ALU.max))
                link(v.tensor_tensor_scan(cum[:], cnt[:], zrow[:], 0.0, ALU.add, ALU.add))
                link(v.tensor_copy(gnum_c[:], gnum_ci[:]))
                link(v.tensor_tensor(diag[:], ident[:, 0:NH], cum[:], ALU.mult))
                link(v.tensor_reduce(end_col[:], diag[:], AX.X, ALU.add))
                v.tensor_scalar(past[:], gnum_c[:], end_col[:, 0:1], None, ALU.is_ge).then_inc(counts_ready, 1)
                dve.wait_ge(sums_ready, 2)
                link(v.tensor_scalar(end_col[:], cum[:, NB - 1:NB], float(TURN - 1), None, ALU.add))
                link(v.tensor_copy(turns_i[:], end_col[:]))
                link(v.tensor_scalar(turns_i[:], turns_i[:], TURN.bit_length() - 1, None, ALU.logical_shift_right))
                link(v.tensor_scalar(c_turns[:, 0:1], turns_i[:], 2, None, ALU.max))
                link(v.tensor_scalar(c_turns[:, 1:2], c_turns[:, 0:1], 1, None, ALU.subtract))
                link(v.tensor_copy(c_block[:], banks[2][:, 0:NGC]))
                link(v.tensor_tensor(cum[:], cum[:], cnt[:], ALU.subtract))
                link(v.scalar_tensor_tensor(first[:], cum[:], float(GC * P), banks[0][:, 0:NH], ALU.mult, ALU.add))

                base2 = done[0]
                with dve.Fori(0, NH) as h:
                    v.tensor_scalar(same[:], hi_bf[:], iota_h[:, bass.ds(h, 1)], None, ALU.is_equal).then_inc(dve_done, 1)
                    dve.wait_ge(dve_done, h * 3 + (base2 + 1))
                    v.tensor_tensor_scan(rank_h[:], same[:], same[:], first[:, bass.ds(h, 1)],
                                         ALU.add, ALU.max).then_inc(dve_done, 1)
                    wait_alone(dve, (dve_done, h * 3 + (base2 + 2)))
                    v.copy_predicated(rank[:], same[:].bitcast(U16), rank_h[:]).then_inc(dve_done, 1)
                    dve.wait_ge(dve_done, h * 3 + (base2 + 3))
                done[0] = base2 + 3 * NH
                link(v.tensor_scalar(rank[:], rank[:], -1.0, None, ALU.add))
                link(v.tensor_copy(hi_i[:], rank[:]))
                link(v.tensor_scalar(dst_i[:], hi_i[:], P - 1, None, ALU.bitwise_and))
                link(v.tensor_scalar(hi_i[:], hi_i[:], 7, None, ALU.logical_shift_right))
                link(v.tensor_copy(rank[:], dst_i[:]))
                link(v.tensor_copy(rank_h[:], hi_i[:]))
                link(v.scalar_tensor_tensor(place[:, :, 3], rank[:], float(RT), rank_h[:], ALU.mult, ALU.add))

        with ExitStack() as ctx:
            rows = sb("rows", [P, GA, W0], F32, ctx)
            hot = sb("hot", [P, GA, P], F32, ctx)
            nodes_here = sb("nodes_here", [P, P], F32, ctx)
            src_slot = [sb(f"src_slot{k}", [P, 1], I32, ctx) for k in range(GA)]
            idx_ready = [sem(f"idx_ready{k}", ctx) for k in range(GA)]
            x_in = [sem(f"x_in{k}", ctx) for k in range(GA)]
            e_in = [sem(f"e_in{k}", ctx) for k in range(GA)]
            summed = [sem(f"summed{k}", ctx) for k in range(GA)]
            hot_ready = sem("hot_ready", ctx)
            nodes_ready = sem("nodes_ready", ctx)
            s_kept = sem("s_kept", ctx)
            block = ctx.enter_context(nc.Block())
            s_ps = banks[0]

            def span(eng, d):
                col = bass.ds(d, 1)
                lo = eng.value_load(a_start[0:1, col], min_val=0, max_val=NG * NB)
                hi = eng.value_load(a_end[0:1, col], min_val=1, max_val=NG * NB)
                skip = eng.value_load(a_skip[0:1, col], min_val=0, max_val=2 * int(FAR))
                return lo, hi, skip

            def tile_of(i, skip, k):
                group = (i + skip - int(FAR)).with_bounds(min_val=0, max_val=NG - 1)
                return group * GA + k

            @block.sync
            def _(sp):
                with sp.Fori(0, NB) as d:
                    lo, hi, skip = span(sp, d)
                    with sp.Fori(lo, hi) as i:
                        for k in range(GA):
                            sp.wait_ge(summed[k], i)
                            sp.dma_start(rows[:, k, D:W0],
                                         a["edge64"][:, bass.ds(tile_of(i, skip, k), 1), :]).then_inc(e_in[k], 16)

            @block.gpsimd
            def _(pool):
                with pool.Fori(0, NB) as d:
                    lo, hi, skip = span(pool, d)
                    with pool.Fori(lo, hi) as i:
                        for k in range(GA):
                            wait_alone(pool, (idx_ready[k], i + 1), (summed[k], i))
                            pool.indirect_dma_start(
                                out=rows[:, k, 0:D], out_offset=None, in_=a["x"],
                                in_offset=bass.IndirectOffsetOnAxis(ap=src_slot[k][:].bitcast(U32), axis=0),
                            ).then_inc(x_in[k], 16)

            @block.scalar
            def _(act):
                with act.Fori(0, NB) as d:
                    lo, hi, skip = span(act, d)
                    with act.Fori(lo, hi) as i:
                        for k in range(GA):
                            act.wait_ge(x_in[k], i * 16)
                            nc.scalar.copy(src_slot[k][:], src_i[:, bass.ds(tile_of(i, skip, k), 1)]).then_inc(idx_ready[k], 1)

            @block.vector
            def _(dve):
                v = nc.vector
                v.tensor_scalar(nodes_here[:], iota[:], -float(P), None, ALU.add).then_inc(nodes_ready, 1)
                with dve.Fori(0, NB) as d:
                    lo, hi, skip = span(dve, d)
                    dve.wait_ge(nodes_ready, d + 1)
                    dve.wait_ge(hot_ready, lo * GA)
                    v.tensor_scalar(nodes_here[:], nodes_here[:], float(P), None, ALU.add).then_inc(nodes_ready, 1)
                    wait_alone(dve, (nodes_ready, d + 2))
                    with dve.Fori(lo, hi) as i:
                        for k in range(GA):
                            dve.wait_ge(summed[k], i)
                            v.tensor_scalar(hot[:, k, :], nodes_here[:], dst_f[:, bass.ds(tile_of(i, skip, k), 1)], None,
                                            ALU.is_equal).then_inc(hot_ready, 1)
                    dve.wait_ge(summed[GA - 1], hi)
                    v.tensor_copy(s_all[:, bass.ds(d, 1), :], s_ps[:, 0:W0].unsqueeze(1)).then_inc(s_kept, 1)

            @block.tensor
            def _(pe):
                with pe.Fori(0, NB) as d:
                    lo, hi, skip = span(pe, d)
                    pe.wait_ge(s_kept, d)
                    nc.tensor.matmul(s_ps[:, 0:W0], zeros_bf[:, 0:P], zeros_bf[:, 0:W0], start=True, stop=False,
                                     skip_group_check=True)
                    with pe.Fori(lo, hi) as i:
                        for k in range(GA):
                            pe.wait_ge(x_in[k], i * 16 + 16)
                            pe.wait_ge(e_in[k], i * 16 + 16)
                            pe.wait_ge(hot_ready, i * GA + (k + 1))
                            nc.tensor.matmul(s_ps[:, 0:W0], hot[:, k, :], rows[:, k, :], start=False, stop=True,
                                             skip_group_check=True).then_inc(summed[k], 1)

        with ExitStack() as ctx:
            w_edge = sb("w_edge", [P, D + 1], F32, ctx)
            b_parts = sb("b_parts", [P, D + 1], BF16, ctx)
            part_f = sb("part_f", [P, D + 1], F32, ctx)
            part_bf = sb("part_bf", [P, D + 1], BF16, ctx)
            ones_bf = sb("ones_bf", [P, P], BF16, ctx)
            row = {n: sb(f"row_{n}", [P, D], F32, ctx) for n in
                   ("a_tgt", "a_nbr", "a_edge", "w_b", "ew_b", "aggr_scale", "aggr_bias", "out_scale", "out_bias")}
            b_edge = sb("b_edge", [P, D + 1], F32, ctx)
            ab_col = sb("ab_col", [P, 1], F32, ctx)
            w_msg = sb("w_msg", [P, KC + 1, D], F32, ctx)
            w_mlp = sb("w_mlp", [P, 3, KC, D], F32, ctx)
            b_mlp = sb("b_mlp", [P, 3, KC], F32, ctx)
            w_node = sb("w_node", [P, KC, D], F32, ctx)
            junk = sb("junk", [P, D], F32, ctx)
            feats = sb("feats", [P, GA, P], F32, ctx)
            relu_y = sb("relu_y", [P, GA, D], F32, ctx)
            rec = [sb(f"rec{k}", [P, GA, REC], I32, ctx) for k in range(GR // GA)]
            x_blk = sb("x_blk", [P, D], F32, ctx)
            s_cur = sb("s_cur", [P, W0], F32, ctx)
            s_t = sb("s_t", [P, (KC + 1) * P], F32, ctx)
            u = sb("u", [P, D], F32, ctx)
            u2 = sb("u2", [P, D], F32, ctx)
            stats = sb("stats", [P, 6], F32, ctx)
            mv = sb("mv", [P, 2], F32, ctx)
            rstd = sb("rstd", [P, 1], F32, ctx)
            std = sb("std", [P, 1], F32, ctx)
            eps = [sb(f"eps{n}", [P, 1], F32, ctx) for n in range(3)]
            h_t = sb("h_t", [P, KC, P], F32, ctx)
            y_t = sb("y_t", [P, KC, P], F32, ctx)
            x1_cur = sb("x1_cur", [P, D], F32, ctx)
            x1_t = sb("x1_t", [P, KC, P], F32, ctx)
            tab = sb("tab", [P, HW], F32, ctx)
            p_cur = sb("p_cur", [P, 1], F32, ctx)

            w_in = sem("w_in", ctx)
            consts = sem("consts", ctx)
            dve_done = sem("dve_done2", ctx)
            f_in = [sem(f"f_in{k}", ctx) for k in range(GA)]
            y_ready = [sem(f"y_ready{k}", ctx) for k in range(GA)]
            relu_ready = [sem(f"relu_ready{k}", ctx) for k in range(GA)]
            rec_ready = sem("rec_ready", ctx)
            logit_ready = [sem(f"logit_ready{k}", ctx) for k in range(GA)]
            rec_out = [sem(f"rec_out{k}", ctx) for k in range(GR)]
            nx = {n: sem("n_" + n, ctx) for n in (
                "x", "s", "sps", "st", "agg", "h0", "h0ps", "h0t", "y0", "y1", "y2", "act0", "act1", "act2",
                "res0", "res1", "res2", "back", "x1", "x1ps", "x1t", "hid", "tab", "tab_out", "dve", "p", "var", "std")}
            block = ctx.enter_context(nc.Block())
            STEPS = NT // GA
            assert PER >= 1
            TR, ND, YT, X1 = banks[4], banks[5], banks[6], banks[7]

            def parts(table, j, d):
                for n, fn in enumerate(table):
                    if min(n, PER - 1) == j:
                        fn(d)

            @block.sync
            def _(sp):
                def load(dst, src):
                    sp.dma_start(dst, src).then_inc(w_in, 16)

                load(w_edge[:, 0:D], a["ew_W"])
                for n, name in enumerate(("a_tgt", "a_nbr", "a_edge")):
                    load(row[name][:], a["a_W"][n:n + 1, :].to_broadcast([P, D]))
                for name in ("w_b", "ew_b", "aggr_scale", "aggr_bias", "out_scale", "out_bias"):
                    load(row[name][:], a[name].to_broadcast([P, D]))
                load(ab_col[:], a["a_b"].to_broadcast([P, 1]))
                for c in range(KC):
                    load(w_msg[:, c, :], a["W_message"][c * P:(c + 1) * P, :])
                    load(w_node[:, c, :], a["w_W"][c * P:(c + 1) * P, :])
                    for n in range(3):
                        load(w_mlp[:, n, c, :], a[f"mlp_W{n}"][c * P:(c + 1) * P, :])
                load(w_msg[0:DE0, KC, :], a["W_message"][D:D + DE0, :])
                for n in range(3):
                    load(b_mlp[:, n, :], a[f"mlp_b{n}"])

                def edge_step(t, j):
                    i = t * 2 + j
                    for k in range(GA):
                        sp.wait_ge(y_ready[k], i)
                        sp.dma_start(feats[:, k, :], a["edge128"][:, bass.ds((i * GA + k) * P, P)]).then_inc(f_in[k], 16)

                def load_x(d):
                    sp.wait_ge(nx["x1"], d)
                    sp.dma_start(x_blk[:], a["x"][bass.ds(d * P, P), :]).then_inc(nx["x"], 16)

                with sp.Fori(0, NB) as d:
                    for j in range(PER):
                        if j == 0:
                            load_x(d)
                        edge_step(d * (PER // 2) + j // 2, j % 2)
                    sp.wait_ge(nx["tab"], d + 1)
                    sp.dma_start(nodetab[bass.ds(d * P, P), :], tab[:]).then_inc(nx["tab_out"], 16)
                with sp.Fori(NB * PER // 2, STEPS // 2) as t:
                    edge_step(t, 0)
                    edge_step(t, 1)
                sp.wait_ge(nx["tab_out"], NB * 16)

            W_LOADS = 1 + 3 + 6 + 1 + KC * 5 + 1 + 3

            @block.gpsimd
            def _(pool):
                with pool.Fori(0, STEPS // 2) as t:
                    for r in range(GR):
                        wait_alone(pool, (logit_ready[r % GA], t * 2 + (r // GA + 1)))
                        pool.indirect_dma_start(
                            out=recs,
                            out_offset=bass.IndirectOffsetOnAxis(ap=rec[r // GA][:, r % GA, 3:4].bitcast(U32), axis=0),
                            in_=rec[r // GA][:, r % GA, :], in_offset=None).then_inc(rec_out[r], 16)
                for r in range(GR):
                    pool.wait_ge(rec_out[r], STEPS // 2 * 16)

            @block.tensor
            def _(pe):
                pe.wait_ge(w_in, W_LOADS * 16)
                pe.wait_ge(consts, 1)
                mm = nc.tensor.matmul

                def edge_step(t, j):
                    i = t * 2 + j
                    for k in range(GA):
                        pe.wait_ge(f_in[k], i * 16 + 16)
                        pe.wait_ge(logit_ready[k], i)
                        mm(banks[k][:, 0:D + 1], feats[:, k, :], w_edge[:], start=True, stop=False)
                        mm(banks[k][:, 0:D + 1], ones_bf[0:3, :], b_parts[0:3, :], start=False, stop=True).then_inc(y_ready[k], 1)

                def turn_s(d):
                    pe.wait_ge(nx["s"], d + 1)
                    for c in range(KC):
                        nc.tensor.transpose(TR[:, c * P:(c + 1) * P], s_cur[:, c * P:(c + 1) * P], ident[:])
                    nc.tensor.transpose(TR[0:DE0, KC * P:(KC + 1) * P], s_cur[:, D:W0], ident[:]).then_inc(nx["sps"], 1)

                def messages(d):
                    pe.wait_ge(nx["st"], d + 1)
                    for c in range(KC):
                        mm(ND[:, 0:D], s_t[:, c * P:(c + 1) * P], w_msg[:, c, :], start=(c == 0), stop=False)
                    mm(ND[:, 0:D], s_t[0:DE0, KC * P:(KC + 1) * P], w_msg[0:DE0, KC, :], start=False,
                       stop=True).then_inc(nx["agg"], 1)

                def turn(out, src, done):
                    for c in range(KC):
                        ins = nc.tensor.transpose(out[:, c * P:(c + 1) * P], src(c), ident[:])
                    ins.then_inc(nx[done], 1)

                def layer(n, before):
                    def fn(d):
                        pe.wait_ge(nx[before], d + 1)
                        for m in range(KC):
                            for c in range(KC):
                                ins = mm(YT[:, m * P:(m + 1) * P], w_mlp[:, n, c, m * P:(m + 1) * P], h_t[:, c, :],
                                         start=(c == 0), stop=(c == KC - 1))
                        ins.then_inc(nx[f"y{n}"], 1)
                    return fn

                def first_layer(d):
                    pe.wait_ge(nx["h0"], d + 1)
                    turn(TR, lambda c: u[:, c * P:(c + 1) * P], "h0ps")
                    layer(0, "h0t")(d)

                def back(d):
                    pe.wait_ge(nx["res2"], d + 1)
                    turn(ND, lambda c: h_t[:, c, :], "back")

                def turn_x1(d):
                    pe.wait_ge(nx["x1"], d + 1)
                    turn(X1, lambda c: x1_cur[:, c * P:(c + 1) * P], "x1ps")

                def hidden(d):
                    pe.wait_ge(nx["x1t"], d + 1)
                    for c in range(KC):
                        ins = mm(ND[:, 0:D], x1_t[:, c, :], w_node[:, c, :], start=(c == 0), stop=(c == KC - 1))
                    ins.then_inc(nx["hid"], 1)

                node = [turn_s, messages, first_layer, layer(1, "res0"), layer(2, "res1"), back, turn_x1, hidden]
                with pe.Fori(0, NB) as d:
                    for j in range(PER):
                        edge_step(d * (PER // 2) + j // 2, j % 2)
                        parts(node, j, d)
                with pe.Fori(NB * PER // 2, STEPS // 2) as t:
                    edge_step(t, 0)
                    edge_step(t, 1)

            @block.scalar
            def _(act):
                act.wait_ge(w_in, W_LOADS * 16)
                act.wait_ge(consts, 1)
                s = nc.scalar

                def edge_step(t, j):
                    i = t * 2 + j
                    for k in range(GA):
                        act.wait_ge(rec_out[j * GA + k], t * 16)
                    s.copy(rec[j][:], place[:, bass.ds(i * GA, GA), :]).then_inc(rec_ready, 1)
                    for k in range(GA):
                        act.wait_ge(y_ready[k], i + 1)
                        s.activation(relu_y[:, k, :], banks[k][:, 0:D], ACT.Relu, scale=1.0 - SLOPE).then_inc(relu_ready[k], 1)

                def take_s(d):
                    act.wait_ge(nx["sps"], d)
                    s.copy(s_cur[:], s_all[:, bass.ds(d, 1), :].squeeze(1)).then_inc(nx["s"], 1)
                    act.wait_ge(nx["sps"], d + 1)
                    s.copy(s_t[:, 0:KC * P], TR[:, 0:KC * P])
                    s.copy(s_t[0:DE0, KC * P:(KC + 1) * P], TR[0:DE0, KC * P:(KC + 1) * P]).then_inc(nx["st"], 1)

                def take_h0(d):
                    act.wait_ge(nx["h0ps"], d + 1)
                    s.copy(h_t[:].rearrange("p c n -> p (c n)"), TR[:, 0:KC * P]).then_inc(nx["h0t"], 1)
                    layer(0)(d)

                def layer(n):
                    def fn(d):
                        act.wait_ge(nx[f"y{n}"], d + 1)
                        for m in range(KC):
                            ins = s.activation(y_t[:, m, :], YT[:, m * P:(m + 1) * P], ACT.Relu if n < 2 else ACT.Identity,
                                               bias=b_mlp[:, n, m:m + 1])
                        ins.then_inc(nx[f"act{n}"], 1)
                    return fn

                def take_x1(d):
                    act.wait_ge(nx["x1ps"], d + 1)
                    s.copy(x1_t[:].rearrange("p c n -> p (c n)"), X1[:, 0:KC * P]).then_inc(nx["x1t"], 1)
                    s.copy(x1_all[:, bass.ds(d, 1), :].squeeze(1), x1_cur[:]).then_inc(nx["p"], 1)

                def take_p(d):
                    act.wait_ge(nx["tab"], d + 1)
                    s.activation(p_all[:, bass.ds(d, 1)], p_cur[:], ACT.Identity, bias=ab_col[:, 0:1]).then_inc(nx["p"], 1)

                def deviation(*norms):
                    def fn(d):
                        for n in norms:
                            act.wait_ge(nx["var"], d * 3 + n + 1)
                            s.activation(std[:], mv[:, 1:2], ACT.Sqrt, bias=eps[n][:, 0:1]).then_inc(nx["std"], 1)
                    return fn

                skip = lambda d: None
                node = [take_s, deviation(0), take_h0, layer(1), layer(2), deviation(1, 2), take_x1, skip, take_p]
                with act.Fori(0, NB) as d:
                    for j in range(PER):
                        edge_step(d * (PER // 2) + j // 2, j % 2)
                        parts(node, j, d)
                with act.Fori(NB * PER // 2, STEPS // 2) as t:
                    edge_step(t, 0)
                    edge_step(t, 1)
                act.wait_ge(nx["p"], 2 * NB)

            @block.vector
            def _(dve):
                v = nc.vector
                done = [0]

                def link(ins):
                    done[0] += 1
                    ins.then_inc(dve_done, 1)
                    dve.wait_ge(dve_done, done[0])

                dve.wait_ge(w_in, W_LOADS * 16)
                link(v.memset(ones_bf[:], 1.0))
                link(v.memset(tab[:], 1.0))
                for n, e in enumerate((LN_EPS, LN_EPS, RES_EPS)):
                    link(v.memset(eps[n][:], e))
                link(v.tensor_tensor_reduce(junk[:], w_edge[:, 0:D], row["a_edge"][:], 1.0, 0.0, ALU.mult, ALU.add,
                                            w_edge[:, D:D + 1]))
                link(v.tensor_copy(b_edge[:, 0:D], row["ew_b"][:]))
                link(v.tensor_tensor_reduce(junk[:], row["ew_b"][:], row["a_edge"][:], 1.0, 0.0, ALU.mult, ALU.add,
                                            b_edge[:, D:D + 1]))
                link(v.tensor_scalar(w_edge[:, D:D + 1], w_edge[:, D:D + 1], SLOPE, None, ALU.mult))
                link(v.tensor_scalar(b_edge[:, D:D + 1], b_edge[:, D:D + 1], SLOPE, None, ALU.mult))
                link(v.memset(b_parts[:], 0.0))
                for n in range(3):
                    link(v.tensor_copy(part_bf[:], b_edge[:]))
                    link(v.tensor_copy(part_f[:], part_bf[:]))
                    link(v.tensor_tensor(b_edge[:], b_edge[:], part_f[:], ALU.subtract))
                    link(v.tensor_scalar(rstd[:], lane[:, 0:1], float(n), None, ALU.is_equal))
                    link(v.scalar_tensor_tensor(b_parts[:], part_f[:], rstd[:, 0:1], b_parts[:], ALU.mult, ALU.add))
                v.memset(junk[:], 0.0).then_inc(consts, 1)

                def edge_step(t, j):
                    i = t * 2 + j
                    dve.wait_ge(rec_ready, i + 1)
                    for k in range(GA):
                        dve.wait_ge(relu_ready[k], i + 1)
                        v.tensor_tensor_reduce(relu_y[:, k, :], relu_y[:, k, :], row["a_edge"][:], 1.0, banks[k][:, D:D + 1],
                                               ALU.mult, ALU.add, rec[j][:, k, 2:3].bitcast(F32)).then_inc(logit_ready[k], 1)

                NDV = 18
                count = [0]

                def step(d, ins):
                    count[0] += 1
                    ins.then_inc(nx["dve"], 1)
                    wait_alone(dve, (nx["dve"], d * NDV + count[0]))

                def normed(d, n, out, src):
                    step(d, v.bn_stats(stats[:], src))
                    v.bn_aggr(mv[:], stats[:]).then_inc(nx["var"], 1)
                    dve.wait_ge(nx["std"], d * 3 + n + 1)
                    step(d, v.reciprocal(rstd[:], std[:]))
                    return v.tensor_scalar(out, src, mv[:, 0:1], rstd[:, 0:1], ALU.subtract, ALU.mult)

                def first_norm(d):
                    dve.wait_ge(nx["agg"], d + 1)
                    dve.wait_ge(nx["x"], d * 16 + 16)
                    step(d, v.scalar_tensor_tensor(u2[:], ND[:, 0:D], 0.0, x_blk[:], ALU.max, ALU.add))
                    step(d, normed(d, 0, u2[:], u2[:]))
                    step(d, v.tensor_tensor(u2[:], u2[:], row["aggr_scale"][:], ALU.mult))
                    v.tensor_tensor(u[:], u2[:], row["aggr_bias"][:], ALU.add).then_inc(nx["h0"], 1)

                def residual(n):
                    def fn(d):
                        dve.wait_ge(nx[f"act{n}"], d + 1)
                        v.tensor_tensor(h_t[:], h_t[:], y_t[:], ALU.add).then_inc(nx[f"res{n}"], 1)
                    return fn

                def out_norms(d):
                    dve.wait_ge(nx["back"], d + 1)
                    step(d, v.tensor_tensor(u2[:], ND[:, 0:D], x_blk[:], ALU.add))
                    step(d, normed(d, 1, u2[:], u2[:]))
                    step(d, v.tensor_tensor(u2[:], u2[:], row["out_scale"][:], ALU.mult))
                    step(d, v.tensor_tensor(u2[:], u2[:], row["out_bias"][:], ALU.add))
                    step(d, v.tensor_tensor(u2[:], u2[:], x_blk[:], ALU.add))
                    dve.wait_ge(nx["p"], d * 2)
                    normed(d, 2, x1_cur[:], u2[:]).then_inc(nx["x1"], 1)

                def table(d):
                    dve.wait_ge(nx["hid"], d + 1)
                    dve.wait_ge(nx["tab_out"], d * 16)
                    step(d, v.tensor_tensor(u2[:], ND[:, 0:D], row["w_b"][:], ALU.add))
                    step(d, v.scalar_tensor_tensor(tab[:, 0:D], u2[:], SLOPE, u2[:], ALU.mult, ALU.max))
                    step(d, v.tensor_tensor_reduce(u2[:], tab[:, 0:D], row["a_nbr"][:], 1.0, 0.0, ALU.mult, ALU.add,
                                                   tab[:, D:D + 1]))
                    step(d, v.tensor_tensor_reduce(u2[:], tab[:, 0:D], row["a_tgt"][:], 1.0, 0.0, ALU.mult, ALU.add,
                                                   p_cur[:]))
                    v.memset(stats[:], 0.0).then_inc(nx["tab"], 1)
                    assert count[0] == NDV, count[0]

                skip = lambda d: None
                node = [skip, first_norm, residual(0), residual(1), residual(2), out_norms, skip, table]
                with dve.Fori(0, NB) as d:
                    for j in range(PER):
                        edge_step(d * (PER // 2) + j // 2, j % 2)
                        parts(node, j, d)
                with dve.Fori(NB * PER // 2, STEPS // 2) as t:
                    edge_step(t, 0)
                    edge_step(t, 1)

        mid.close()

        o_all = sb("o_all", [P, NH, HW])
        with ExitStack() as ctx:
            recs_sb = sb("recs_sb", [P, RT, REC], I32, ctx)
            lane_f = sb("lane_f", [P, RT], F32, ctx)
            nbr_all = sb("nbr_all", [P, RT], I32, ctx)
            nbr = sb("nbr", [P, TURN * GC, HW], F32, ctx)
            nbr_idx = [sb(f"nbr_idx{u}", [P, GC], I32, ctx) for u in range(TURN)]
            logit = [sb(f"logit{u}", [P, GC], F32, ctx) for u in range(TURN)]
            off = sb("off", [P, TURN * GC, P], BF16, ctx)
            iota_bf = sb("iota_bf", [P, P], BF16, ctx)
            w = sb("w", [P, TURN * GC, P], F32, ctx)
            m_diag = [sb(f"m_diag{u}", [P, P], F32, ctx) for u in range(2)]
            m_all = sb("m_all", [P, NH], F32, ctx)
            best = [sb(f"best{u}", [P, 1], F32, ctx) for u in range(TURN)]
            m_new = [sb(f"m_new{u}", [P, 1], F32, ctx) for u in range(TURN)]
            m_rest = [sb(f"m_rest{u}", [P, 1], F32, ctx) for u in range(TURN)]
            decay = [sb(f"decay{u}", [P, 1], F32, ctx) for u in range(TURN)]
            T_PS, M_PS, O_PS = banks[0:2], banks[2:4], banks[4:6]

            recs_in = sem("recs_in", ctx)
            split = sem("split", ctx)
            idx_in = [sem(f"idx_in{u}", ctx) for u in range(TURN)]
            nbr_in = [sem(f"nbr_in{k}", ctx) for k in range(TURN * GC)]

            def sems(name):
                return [sem(f"{name}{u}", ctx) for u in range(TURN)]

            summed = sems("weighted")
            logit_ready = sems("lg_ready")
            x_ready = sems("x_ready")
            turned = sems("turned")
            max_steps = sems("max_steps")
            m_row = sems("m_row")
            decay_steps = sems("decay_steps")
            below_ready = sems("below_ready")
            w_ready = sems("w_ready")
            added = sems("added")
            block = ctx.enter_context(nc.Block())
            BEST, NEW, REST, DIAG = (4, 1), (4, 2), (4, 3), (4, 4)
            DECAY, KEPT = (2, 1), (2, 2)

            def back(i, u, n):
                return (i, u - n) if u >= n else (i - 1, u - n + TURN)

            def wait_group(eng, sems, i, u, n=0, step=(1, 1)):
                i, u = back(i, u, n)
                eng.wait_ge(sems[u], i * step[0] + step[1])

            def turns(eng, step):
                n = eng.value_load(c_turns[0:1, 0:1], min_val=2, max_val=NGC // TURN)
                last = eng.value_load(c_turns[0:1, 1:2], min_val=1, max_val=NGC // TURN)
                for u in range(TURN):
                    step(0, u, first=min(u, 2), ends=0)
                with eng.Fori(1, n) as i:
                    for u in range(TURN):
                        step(i, u, first=2, ends=0)
                for u in range(2):
                    step(last, TURN + u, first=2, ends=u + 1)

            def block_of(eng, i, u):
                at = i.with_bounds(min_val=0, max_val=NGC // TURN - 1) if not isinstance(i, int) else i
                return eng.value_load(c_block[0:1, bass.ds(at * TURN + u, 1)], min_val=0, max_val=NB)

            def tile0(i, u):
                at = i.with_bounds(min_val=0, max_val=NGC // TURN - 1) if not isinstance(i, int) else i
                return at * (TURN * GC) + u * GC

            @block.sync
            def _(sp):
                sp.dma_start(recs_sb[:], recs_pt).then_inc(recs_in, 16)
                sp.wait_ge(split, 2)
                n = sp.value_load(c_turns[0:1, 0:1], min_val=2, max_val=NGC // TURN)
                with sp.Fori(0, n) as i:
                    for u in range(TURN):
                        for k in range(GC):
                            sp.wait_ge(nbr_in[u * GC + k], i * 16)
                        sp.dma_start(nbr_idx[u][:], nbr_all[:, bass.ds(tile0(i, u), GC)]).then_inc(idx_in[u], 16)

            @block.gpsimd
            def _(pool):
                n = pool.value_load(c_turns[0:1, 0:1], min_val=2, max_val=NGC // TURN)
                with pool.Fori(0, n) as i:
                    for u in range(TURN):
                        for k in range(GC):
                            wait_alone(pool, (idx_in[u], i * 16 + 16), (summed[u], i))
                            pool.indirect_dma_start(
                                out=nbr[:, u * GC + k, :], out_offset=None, in_=nodetab,
                                in_offset=bass.IndirectOffsetOnAxis(ap=nbr_idx[u][:, k:k + 1].bitcast(U32), axis=0),
                            ).then_inc(nbr_in[u * GC + k], 16)

            @block.tensor
            def _(pe):
                mm = nc.tensor.matmul

                def row(i, u):
                    wait_group(pe, max_steps, i, u, step=DIAG)
                    mm(M_PS[u % 2][:, 0:P], ones[:], m_diag[u % 2][:], start=True, stop=True).then_inc(m_row[u], 1)

                def turn(i, u, first):
                    wait_group(pe, x_ready, i, u)
                    if first >= 2:
                        wait_group(pe, max_steps, i, u, 2, BEST)
                    for k in range(GC):
                        ins = nc.tensor.transpose(T_PS[u % 2][:, k * P:(k + 1) * P], w[:, u * GC + k, :], ident[:])
                    ins.then_inc(turned[u], 1)

                def weigh(i, u, first):
                    wait_group(pe, w_ready, i, u)
                    if first >= 2:
                        wait_group(pe, added, i, u, 2)
                    for k in range(GC):
                        ins = mm(O_PS[u % 2][:, 0:HW], w[:, u * GC + k, :], nbr[:, u * GC + k, :], start=(k == 0),
                                 stop=(k == GC - 1))
                    ins.then_inc(summed[u], 1)

                def step(i, u, first, ends):
                    if first >= 1 and ends < 2:
                        row(*back(i, u, 1))
                    if not ends:
                        turn(i, u, 2 if not isinstance(i, int) else u)
                    if first >= 1 and ends < 2:
                        bi, bu = back(i, u, 1)
                        weigh(bi, bu, 2 if not isinstance(i, int) else bu)

                turns(pe, step)

            @block.scalar
            def _(act):
                s = nc.scalar

                def place_logits(i, u):
                    wait_group(act, logit_ready, i, u)
                    act.wait_ge(summed[u], i)
                    for k in range(GC):
                        ins = s.activation(w[:, u * GC + k, :], off[:, u * GC + k, :], ACT.Identity,
                                           bias=logit[u][:, k:k + 1])
                    ins.then_inc(x_ready[u], 1)

                def decays(i, u):
                    wait_group(act, max_steps, i, u, step=NEW)
                    here = m_all[:, bass.ds(block_of(act, i, u), 1)]
                    s.activation(decay[u][:], m_new[u][:], ACT.Exp, scale=-1.0, bias=here).then_inc(decay_steps[u], 1)
                    wait_alone(act, (decay_steps[u], i * DECAY[0] + DECAY[1]))
                    s.activation(here, m_new[u][:], ACT.Identity).then_inc(decay_steps[u], 1)

                def weights(i, u):
                    wait_group(act, below_ready, i, u)
                    group = w[:, u * GC:(u + 1) * GC, :]
                    s.activation(group, group, ACT.Exp).then_inc(w_ready[u], 1)

                def step(i, u, first, ends):
                    if not ends:
                        place_logits(i, u)
                    if first >= 1 and ends < 2:
                        decays(*back(i, u, 1))
                        weights(*back(i, u, 1))

                turns(act, step)

            @block.vector
            def _(dve):
                v = nc.vector
                v.memset(m_all[:], LOWEST)
                v.memset(o_all[:], 0.0)
                v.tensor_copy(iota_bf[:], iota[:])
                dve.wait_ge(recs_in, 16)
                v.tensor_copy(lane_f[:], recs_sb[:, :, 0]).then_inc(split, 1)
                v.tensor_copy(nbr_all[:], recs_sb[:, :, 1]).then_inc(split, 1)
                dve.wait_ge(split, 2)

                def mask(i, u):
                    dve.wait_ge(x_ready[u], i)
                    for k in range(GC):
                        v.tensor_scalar(off[:, u * GC + k, :], iota_bf[:], lane_f[:, bass.ds(tile0(i, u) + k, 1)], MASKED,
                                        ALU.not_equal, ALU.mult)

                def logits(i, u):
                    for k in range(GC):
                        dve.wait_ge(nbr_in[u * GC + k], (i + 1) * 16)
                    v.tensor_tensor(logit[u][:], recs_sb[:, bass.ds(tile0(i, u), GC), 2].bitcast(F32),
                                    nbr[:, u * GC:(u + 1) * GC, D], ALU.add).then_inc(logit_ready[u], 1)

                def maximum(i, u, first):
                    wait_group(dve, turned, i, u)
                    v.tensor_reduce(best[u][:], T_PS[u % 2][:, :], AX.X, ALU.max).then_inc(max_steps[u], 1)
                    d = block_of(dve, i, u)
                    p_here = p_all[:, bass.ds(d, 1)]
                    wait_group(dve, max_steps, i, u, step=BEST)
                    if first:
                        wait_group(dve, decay_steps, i, u, 1, KEPT)
                    v.scalar_tensor_tensor(m_new[u][:], best[u][:], p_here, m_all[:, bass.ds(d, 1)], ALU.add,
                                           ALU.max).then_inc(max_steps[u], 1)
                    wait_group(dve, max_steps, i, u, step=NEW)
                    v.tensor_tensor(m_rest[u][:], m_new[u][:], p_here, ALU.subtract).then_inc(max_steps[u], 1)
                    wait_group(dve, max_steps, i, u, step=REST)
                    v.tensor_scalar(m_diag[u % 2][:], ident[:], m_rest[u][:, 0:1], None, ALU.mult).then_inc(max_steps[u], 1)

                def below(i, u):
                    wait_group(dve, m_row, i, u)
                    group = w[:, u * GC:(u + 1) * GC, :]
                    v.tensor_tensor(group, group, M_PS[u % 2][:, 0:P].unsqueeze(1).to_broadcast([P, GC, P]),
                                    ALU.subtract).then_inc(below_ready[u], 1)

                def add(i, u, first):
                    here = o_all[:, bass.ds(block_of(dve, i, u), 1), :].squeeze(1)
                    wait_group(dve, summed, i, u)
                    wait_group(dve, decay_steps, i, u, step=DECAY)
                    if first:
                        wait_group(dve, added, i, u, 1)
                    v.scalar_tensor_tensor(here, here, decay[u][:, 0:1], O_PS[u % 2][:, 0:HW], ALU.mult,
                                           ALU.add).then_inc(added[u], 1)

                def step(i, u, first, ends):
                    early = isinstance(i, int)
                    if first >= 1 and ends < 2:
                        maximum(*back(i, u, 1), first=not early or u > 1)
                    if not ends:
                        mask(i, u)
                        logits(i, u)
                    if first >= 1 and ends < 2:
                        below(*back(i, u, 1))
                    if first >= 2:
                        add(*back(i, u, 2), first=not early or u > 2)

                turns(dve, step)

        with ExitStack() as ctx:
            den = sb("den", [P, 1], F32, ctx)
            inv = sb("inv", [P, 1], F32, ctx)
            y = sb("y", [P, D], F32, ctx)
            y2 = sb("y2", [P, D], F32, ctx)
            res = [sb(f"res{b}", [P, D], F32, ctx) for b in range(2)]
            stats = sb("stats_f", [P, 6], F32, ctx)
            mv = sb("mv_f", [P, 2], F32, ctx)
            std = sb("std_f", [P, 1], F32, ctx)
            eps = sb("eps_f", [P, 1], F32, ctx)
            var_ready = sem("var_ready", ctx)
            std_ready = sem("std_ready", ctx)
            eps_ready = sem("eps_ready", ctx)
            res_ready = sem("res_ready", ctx)
            out_done = sem("out_done", ctx)
            step_done = sem("step_done", ctx)
            block = ctx.enter_context(nc.Block())
            LAST = n_nodes - (NB - 1) * P

            @block.sync
            def _(sp):
                with sp.Fori(0, NB - 1) as d:
                    sp.wait_ge(res_ready, d + 1)
                    sp.dma_start(a["out"][bass.ds(d * P, P), :], res[0][:]).then_inc(out_done, 16)
                sp.wait_ge(res_ready, NB)
                sp.dma_start(a["out"][(NB - 1) * P:n_nodes, :], res[0][0:LAST, :]).then_inc(out_done, 16)
                sp.wait_ge(out_done, NB * 16)

            @block.scalar
            def _(act):
                act.wait_ge(eps_ready, 1)
                with act.Fori(0, NB) as d:
                    act.wait_ge(var_ready, d + 1)
                    nc.scalar.activation(std[:], mv[:, 1:2], ACT.Sqrt, bias=eps[:, 0:1]).then_inc(std_ready, 1)

            @block.vector
            def _(dve):
                v = nc.vector
                v.memset(eps[:], RES_EPS).then_inc(eps_ready, 1)
                NDV = 7
                with dve.Fori(0, NB) as d:
                    count = [0]

                    def step(ins):
                        count[0] += 1
                        ins.then_inc(step_done, 1)
                        wait_alone(dve, (step_done, d * NDV + count[0]))

                    row_d = bass.ds(d, 1)
                    step(v.tensor_scalar(den[:], o_all[:, row_d, D + 1], 1e-30, None, ALU.max))
                    step(v.reciprocal(inv[:], den[:]))
                    step(v.tensor_scalar(y[:], o_all[:, row_d, 0:D].squeeze(1), inv[:, 0:1], None, ALU.mult))
                    step(v.scalar_tensor_tensor(y2[:], y[:], SLOPE, y[:], ALU.mult, ALU.max))
                    step(v.tensor_tensor(y[:], y2[:], x1_all[:, row_d, :].squeeze(1), ALU.add))
                    step(v.bn_stats(stats[:], y[:]))
                    v.bn_aggr(mv[:], stats[:]).then_inc(var_ready, 1)
                    dve.wait_ge(std_ready, d + 1)
                    step(v.reciprocal(inv[:], std[:]))
                    dve.wait_ge(out_done, d * 16)
                    v.tensor_scalar(res[0][:], y[:], mv[:, 0:1], inv[:, 0:1], ALU.subtract, ALU.mult).then_inc(res_ready, 1)
                    assert count[0] == NDV, count[0]


def layout(f):
    import numpy as np

    f = {k: np.asarray(v) for k, v in f.items()}
    n_nodes, n_edges = f["x"].shape[0], f["src"].shape[0]
    z = sizes(n_nodes, n_edges)
    none = z["blocks"] * P
    more = z["tiles"] * P - n_edges

    def lanes(v):
        return np.ascontiguousarray(np.pad(v, (0, more), constant_values=none).reshape(-1, P).T)

    groups = np.pad(f["dst"], (0, z["gp"] * P * GA * P - n_edges), constant_values=none)
    e64 = np.pad(f["edge_attr_64"], ((0, more), (0, 0)))
    ins = dict(
        x=np.pad(f["x"], ((0, none + P - n_nodes), (0, 0))),
        src=lanes(f["src"]),
        dst=lanes(f["dst"]),
        dst_groups=groups.reshape(P, z["gp"], GA * P),
        edge64=np.ascontiguousarray(e64.reshape(z["tiles"], P, -1).transpose(1, 0, 2)),
        edge128=np.ascontiguousarray(np.pad(f["edge_attr_128"], ((0, more), (0, 0))).T),
        W_message=f["L0_gnn_W_message"],
        a_W=f["L1_gnn_a_W"].reshape(3, -1),
        a_b=f["L1_gnn_a_b"].reshape(1, 1),
        w_W=f["L1_gnn_w_W"],
        ew_W=f["L1_gnn_ew_W"],
        w_b=f["L1_gnn_w_b"].reshape(1, -1),
        ew_b=f["L1_gnn_ew_b"].reshape(1, -1),
    )
    for n in range(3):
        ins[f"mlp_W{n}"] = f[f"L0_gnn_mlp_W{n}"]
        ins[f"mlp_b{n}"] = np.ascontiguousarray(f[f"L0_gnn_mlp_b{n}"].reshape(-1, P).T)
    for n in ("aggr_scale", "aggr_bias", "out_scale", "out_bias"):
        ins[n] = f[f"L0_gnn_ln_{n}"].reshape(1, -1)
    return ins


def kernel(**inputs):
    import numpy as np
    import concourse.bacc as bacc
    from concourse.bass_utils import run_bass_kernel_spmd

    n_nodes, n_edges = inputs["x"].shape[0], inputs["src"].shape[0]
    arrays = {k: np.ascontiguousarray(v) for k, v in layout(inputs).items()}
    nc = bacc.Bacc("TRN2", target_bir_lowering=False, num_devices=1)
    a = {k: nc.dram_tensor(f"in_{k}", v.shape, mybir.dt.from_np(v.dtype), kind="ExternalInput").ap()
         for k, v in arrays.items()}
    a["out"] = nc.dram_tensor("out", inputs["x"].shape, F32, kind="ExternalOutput").ap()
    build(nc, a, n_nodes, n_edges)
    r = run_bass_kernel_spmd(nc, [{f"in_{k}": v for k, v in arrays.items()}], core_ids=[0])
    return r.results[0]["out"]
```
